# Optimizing a Trainium2 kernel written in Bass

```python
import numpy as np
import jax
import jax.numpy as jnp

def _softmax(x, axis=-1):
    return jax.nn.softmax(x, axis=axis)
def _gelu(x):
    return jax.nn.gelu(x, approximate=True)
def _silu(x):
    return jax.nn.silu(x)
def _sigmoid(x):
    return jax.nn.sigmoid(x)
def _layernorm(x, axis=-1, eps=1e-5):
    m = jnp.mean(x, axis=axis, keepdims=True)
    v = jnp.var(x, axis=axis, keepdims=True)
    return (x - m) / jnp.sqrt(v + eps)
def _scatter_add(tgt, idx, src, axis=0):
    return tgt.at[idx].add(src)
def _segment_sum(src, seg, n):
    return jax.ops.segment_sum(src, seg, n)

kernel_name = 'mk_adj_preln_d1_adj_256_972561'

def setup_inputs(seed: int = 0):
    np.random.seed(seed)
    _w = jnp.asarray
    def _rec_inputs():
        import jax
        import jax.numpy as jnp
        _gk = jax.random.key(seed)
        x = -0.0005207 + 1.001 * jax.random.normal(jax.random.fold_in(_gk, 1), (8192, 256), jnp.float32)
        _a = jax.random.bernoulli(jax.random.fold_in(_gk, 2), 0.000976562, (8192, 8192))
        adj = _a.astype(jnp.int32)
        return x, adj
    x, adj = _rec_inputs()
    def _L0_gnn_setup():
        import jax, jax.numpy as jnp
        import numpy as np
        MIN_NORM = 1e-15
        EPS = 1e-07
        MASK_FILL = -9000000000000000.0

        def logmap0(x, c):
            K = 1.0 / c
            sqrtK = K ** 0.5
            y = x[:, 1:]
            y_norm = jnp.clip(jnp.linalg.norm(y, axis=-1, keepdims=True), MIN_NORM)
            theta = jnp.clip(x[:, :1] / sqrtK, 1.0 + EPS)
            res = sqrtK * jnp.arccosh(theta) * y / y_norm
            return jnp.concatenate([jnp.zeros_like(x[:, :1]), res], axis=1)

        def proj(x, c):
            K = 1.0 / c
            y = x[:, 1:]
            x0 = jnp.sqrt(K + jnp.sum(y * y, axis=-1, keepdims=True))
            return jnp.concatenate([x0, y], axis=1)

        def expmap0(u, c):
            K = 1.0 / c
            sqrtK = K ** 0.5
            x = u[:, 1:]
            x_norm = jnp.clip(jnp.linalg.norm(x, axis=-1, keepdims=True), MIN_NORM)
            theta = x_norm / sqrtK
            res = jnp.concatenate([sqrtK * jnp.cosh(theta), sqrtK * jnp.sinh(theta) * x / x_norm], axis=1)
            return proj(res, c)
        key = jax.random.key(seed)
        k1, k2, k3, k4, k5 = jax.random.split(key, 5)
        N, D_in, D_out = (8192, 256, 256)
        x = jax.random.normal(k1, (N, D_in), dtype=jnp.float32)
        adj = jax.random.randint(k2, (N, N), 0, 2, dtype=jnp.int32)
        W_gcn = jax.random.normal(k3, (D_in - 1, D_out - 1), dtype=jnp.float32)
        std_w = 1.414 * (2.0 / (D_out + D_out)) ** 0.5
        W_att = jax.random.normal(k4, (D_out, D_out), dtype=jnp.float32) * std_w
        std_a = 1.414 * (2.0 / (2 * D_out + 1)) ** 0.5
        a_att = jax.random.normal(k5, (2 * D_out, 1), dtype=jnp.float32) * std_a
        return {'x': x, 'adj': adj, 'k': 1, 'W_gcn': W_gcn, 'W_att': W_att, 'a_att': a_att}
    _L0_gnn_all = _L0_gnn_setup()
    _L0_gnn_in = {k: v for k, v in _L0_gnn_all.items() if k in ('W_gcn', 'W_att', 'a_att', )}
    del _L0_gnn_all

    return {
        "x": x,
        "adj": adj,
        "L0_gnn_W_gcn": _L0_gnn_in["W_gcn"],
        "L0_gnn_W_att": _L0_gnn_in["W_att"],
        "L0_gnn_a_att": _L0_gnn_in["a_att"],
    }

def reference(x, adj, L0_gnn_W_gcn, L0_gnn_W_att, L0_gnn_a_att):
    import jax
    import jax.numpy as jnp
    def _L0_gnn_ref(x, adj, k, W_gcn, W_att, a_att):
        import jax, jax.numpy as jnp
        import numpy as np
        MIN_NORM = 1e-15
        EPS = 1e-07
        MASK_FILL = -9000000000000000.0

        def logmap0(x, c):
            K = 1.0 / c
            sqrtK = K ** 0.5
            y = x[:, 1:]
            y_norm = jnp.clip(jnp.linalg.norm(y, axis=-1, keepdims=True), MIN_NORM)
            theta = jnp.clip(x[:, :1] / sqrtK, 1.0 + EPS)
            res = sqrtK * jnp.arccosh(theta) * y / y_norm
            return jnp.concatenate([jnp.zeros_like(x[:, :1]), res], axis=1)

        def proj(x, c):
            K = 1.0 / c
            y = x[:, 1:]
            x0 = jnp.sqrt(K + jnp.sum(y * y, axis=-1, keepdims=True))
            return jnp.concatenate([x0, y], axis=1)

        def expmap0(u, c):
            K = 1.0 / c
            sqrtK = K ** 0.5
            x = u[:, 1:]
            x_norm = jnp.clip(jnp.linalg.norm(x, axis=-1, keepdims=True), MIN_NORM)
            theta = x_norm / sqrtK
            res = jnp.concatenate([sqrtK * jnp.cosh(theta), sqrtK * jnp.sinh(theta) * x / x_norm], axis=1)
            return proj(res, c)
        c = float(k)
        N = x.shape[0]
        logx = logmap0(x, c)
        Wx = logx[:, 1:] @ W_gcn
        tmp = jnp.concatenate([jnp.zeros((N, 1), x.dtype), Wx], axis=1)
        fun7 = proj(expmap0(tmp, c), c)
        h_in = logmap0(fun7, c)
        h = h_in @ W_att
        F_ = h.shape[1]
        e = h @ a_att[:F_] + (h @ a_att[F_:]).T
        att = jnp.where(adj > 0, e, MASK_FILL)
        att = jax.nn.softmax(att, axis=1)
        h_prime = att @ h
        emb = jax.nn.elu(h_prime)
        emb = proj(emb, c)
        out = expmap0(jax.nn.sigmoid(logmap0(emb, c)), c)
        return out

    h = jnp.maximum(_layernorm(x, axis=-1), 0.0)
    x = x + _L0_gnn_ref(h, adj, 1, L0_gnn_W_gcn, L0_gnn_W_att, L0_gnn_a_att)
    return x


_drawn_inputs = setup_inputs


def setup_inputs(seed=0):
    import zlib

    import numpy as np

    out = dict(_drawn_inputs(seed))
    spreads = {}
    factors = {}
    for name, (base, spread) in spreads.items():
        noise = np.random.default_rng([zlib.crc32(name.encode()), seed]).standard_normal(out[name].shape)
        drawn = base * np.exp(spread * noise) if base else spread * noise
        out[name] = jnp.asarray(drawn.astype(out[name].dtype))
    for name, factor in factors.items():
        out[name] = (out[name] * factor).astype(out[name].dtype)
    return out
```

```python
import math
from contextlib import ExitStack

import concourse.bass as bass
from concourse import mybir


ALU = mybir.AluOpType
ACT = mybir.ActivationFunctionType
AX = mybir.AxisListType
F32 = mybir.dt.float32
BF16 = mybir.dt.bfloat16
F16 = mybir.dt.float16
U32 = mybir.dt.uint32
I32 = mybir.dt.int32

P = 128
QUAD = 4
B32 = P // QUAD
LN_EPS = 1e-5
NORM_FLOOR2 = 1e-30
THETA_MIN = 1.0 + 2.0 ** -23
ACOSH_MIN = math.acosh(THETA_MIN)
EXP_MASK = 0x7F800000
BETA = 2.0 ** -14
SQRT_MAGIC = float(0x1FBD1DF5)


class Chain:

    def __init__(self, eng, sem, base):
        self.eng, self.sem, self.base, self.n = eng, sem, base, 0

    def __call__(self, ins):
        ins.then_inc(self.sem, 1)
        self.n += 1
        self.eng.wait_ge(self.sem, self.base + self.n)


def gnn_kernel(nc, x, adj, w_gcn, w_att, a_att, out):
    N, D = x.shape
    DH = D // P
    NQ = N // QUAD
    TILES = N // P
    PAIRS = TILES // 2
    CHUNKS = 4
    CT = TILES // CHUNKS
    CP = CT // 2
    IB = 512
    BLOCKS = N // IB
    G32 = IB // B32
    QTR = 4
    QN = NQ // QTR
    UNITS = 2 * QTR
    UT = TILES // UNITS
    UM = UT // 2
    SLOTS = 2 * UT
    RT = IB // P

    with ExitStack() as ctx:
        def sb(name, shape, dt):
            return ctx.enter_context(nc.sbuf_tensor(name, shape, dt))

        def pb(name, shape, dt=F32):
            return ctx.enter_context(nc.psum_tensor(name, shape, dt))

        def sem(name):
            return ctx.enter_context(nc.semaphore(name))

        xz = sb("xz", [P, TILES * D], F32)
        xz_t = xz[:, :].rearrange("p (t d) -> p t d", d=D)
        LOADF = G32 * QN // 2
        raw0 = sb("raw0", [P, G32 * QN], BF16)
        raw = [raw0[:, :]] + [xz[:, i * LOADF:(i + 1) * LOADF].bitcast(BF16) for i in range(QTR - 1)]
        rest = (QTR - 1) * LOADF
        uT = xz[:, rest:rest + DH * IB].rearrange("p (h i) -> p h i", h=DH)
        hrow = xz[:, rest + DH * IB:rest + DH * IB + RT * D].rearrange("p (k d) -> p k d", d=D)
        erow = [xz[:, rest + DH * IB + (1 + b) * RT * D:rest + DH * IB + (2 + b) * RT * D]
                .rearrange("p (k d) -> p k d", d=D) for b in range(2)]
        gbuf = sb("gbuf", [P, TILES * 2 * D], F16)
        g = gbuf[:, :].rearrange("p (t s d) -> p t s d", s=2, d=D)
        ring = gbuf[:, 0:4 * 4 * D * 2].bitcast(F32)
        hb = [ring[:, i * 2 * D:(i + 1) * 2 * D].rearrange("p (e d) -> p e d", e=2) for i in range(2)]
        hT = [ring[:, (2 + i) * 2 * D:(3 + i) * 2 * D].rearrange("p (h e j) -> p h e j", h=DH, e=2) for i in range(2)]
        mT = [sb(f"mT{i}", [P, UM, G32, B32], U32) for i in range(2)]
        ms = sb("ms", [P, SLOTS, IB], BF16)
        xt = [sb(f"xt{i}", [P, RT, D], F32) for i in range(2)]
        wg = sb("wg", [P, DH, D], F32)
        wa = sb("wa", [P, DH, D + 1], F32)
        was = sb("was", [P, DH, D], F32)
        a2b = sb("a2b", [P, D], F32)
        ub = sb("ub", [P, D], F32)
        ident = sb("ident", [P, P], F32)
        ones = sb("ones", [P, P], F32)
        diag = sb("diag", [P, DH, P], F32)
        hmean = sb("hmean", [P, D], F32)
        junk_h = sb("junk_h", [P, D], F32)
        junk_v = sb("junk_v", [P, D], F32)
        junk_a = sb("junk_a", [P, D], F32)
        st = sb("st", [P, CT, 6], F32)
        c16 = sb("c16", [P, 8, CT], F32)
        s64 = sb("s64", [P, 16, TILES], F32)
        (rstd, nbias, q0, ny2, n2, c_, n_, a_, r_, w_, beta, gs, gr, tv, tmp64, tmp65) = [s64[:, i, :] for i in range(16)]
        sc = sb("sc", [P, 16], F32)
        e8 = sb("e8", [P, 16, 8], F32)

        acc = [[pb(f"acc{b}{h}", [P, IB]) for h in range(DH)] for b in range(2)]
        hp = [pb(f"hp{i}", [P, 512]) for i in range(2)]
        pm = pb("pm", [P, 512])
        pm2 = pb("pm2", [P, 512])
        hTp = [acc[0][i] for i in range(2)]
        zp = [acc[1][i] for i in range(2)]

        consts_set = sem("consts_set")
        ident_cleared = sem("ident_cleared")
        weights_loaded = sem("weights_loaded")
        x_loaded = sem("x_loaded")
        prep_ready = sem("prep_ready")
        prep_multiplied = sem("prep_multiplied")
        var_ready = sem("var_ready")
        sd_ready = sem("sd_ready")
        stats_ready = sem("stats_ready")
        h_ready = sem("h_ready")
        h_transposed = sem("h_transposed")
        h_squared = sem("h_squared")
        hT_copied = sem("hT_copied")
        z_multiplied = sem("z_multiplied")
        z_copied = sem("z_copied")
        z_squared = sem("z_squared")
        v_step = sem("v_step")
        r_ready = sem("r_ready")
        v_chunk = sem("v_chunk")
        v_norm = sem("v_norm")
        v_root = sem("v_root")
        v_scale = sem("v_scale")
        v_sig = sem("v_sig")
        v_fin = sem("v_fin")
        a_step = sem("a_step")
        node_v = sem("node_v")
        node_a = sem("node_a")
        node_p = sem("node_p")
        mean_sum = sem("mean_sum")
        w_ready = sem("w_ready")
        gh_ready = sem("gh_ready")
        gl_ready = sem("gl_ready")
        g0_ready = sem("g0_ready")
        adj_loaded = [sem(f"adj_loaded{i}") for i in range(QTR)]
        is_set = sem("is_set")
        transposed = sem("transposed")
        scaled = sem("scaled")
        multiplied = sem("multiplied")
        acc_copied = sem("acc_copied")
        projected = sem("projected")
        hp_read = sem("hp_read")
        neg_ready = sem("neg_ready")
        exp_ready = sem("exp_ready")
        elu_ready = sem("elu_ready")
        elu_squared = sem("elu_squared")
        ln_arg = sem("ln_arg")
        ln_ready = sem("ln_ready")
        scale_ready = sem("scale_ready")
        tanh_ready = sem("tanh_ready")
        norm_ready = sem("norm_ready")
        cosh_ready = sem("cosh_ready")
        rows_ready = sem("rows_ready")
        xt_loaded = [sem(f"xt_loaded{i}") for i in range(2)]
        stored = [sem(f"stored{i}") for i in range(2)]

        x_nodes = x.rearrange("(a m w e) d -> a w m (e d)", a=QUAD, w=B32, e=2)
        x_rows = x.rearrange("(b k p) d -> b p k d", k=RT, p=P)
        out_rows = out.rearrange("(b k p) d -> b p k d", k=RT, p=P)
        adj_v = adj.rearrange("(b g i) (a n) -> b a i g n", g=G32, i=B32, a=QUAD)
        VCH = 8
        N_NORM, N_ROOT, N_SCALE, N_SIG, N_FIN = 16, 12, 2, 2 * 4 + 11, 4

        block = ctx.enter_context(nc.Block())

        @block.sync
        def _(sp):
            sp.wait_ge(consts_set, 6)
            sp.dma_start(wg[1:P, 0, 0:D - 1], w_gcn[0:P - 1, :]).then_inc(weights_loaded, 16)
            sp.dma_start(wg[:, 1, 0:D - 1], w_gcn[P - 1:D - 1, :]).then_inc(weights_loaded, 16)
            sp.dma_start(wa[1:P, 0, 0:D], w_att[1:P, :]).then_inc(weights_loaded, 16)
            sp.dma_start(wa[:, 1, 0:D], w_att[P:D, :]).then_inc(weights_loaded, 16)
            sp.dma_start(was[:, 0, :], w_att[1:P + 1, :]).then_inc(weights_loaded, 16)
            sp.dma_start(was[0:P - 1, 1, :], w_att[P + 1:D, :]).then_inc(weights_loaded, 16)
            sp.dma_start(a2b[:, :], a_att[D:2 * D, :].rearrange("d o -> o d").to_broadcast([P, D])).then_inc(weights_loaded, 16)
            with sp.Fori(0, CHUNKS) as c:
                sp.wait_ge(x_loaded, c * (16 * QUAD))
                for a in range(QUAD):
                    dst = xz_t[a * B32:(a + 1) * B32, bass.ts(c, CT), :]
                    sp.dma_start(dst.rearrange("p (m e) d -> p m (e d)", e=2),
                                 x_nodes[a, :, bass.ts(c, CP), :]).then_inc(x_loaded, 16)

            def load_rows(j, b):
                sp.dma_start(xt[b][:, :, :], x_rows[j, :, :, :]).then_inc(xt_loaded[b], 16)

            def store_rows(j, b):
                sp.wait_ge(rows_ready, j + 1)
                sp.dma_start(out_rows[j, :, :, :], xt[b][:, :, :]).then_inc(stored[b], 16)

            load_rows(0, 0)
            load_rows(1, 1)
            with sp.Fori(0, BLOCKS // 2 - 1) as k:
                for b in range(2):
                    store_rows(2 * k + b, b)
                    sp.wait_ge(stored[b], 16 * (k + 1))
                    load_rows(2 * k + 2 + b, b)
            for b in range(2):
                store_rows(BLOCKS - 2 + b, b)
            for b in range(2):
                sp.wait_ge(stored[b], 16 * (BLOCKS // 2))

        @block.gpsimd
        def _(pool):
            pool.memset(ident[:, :], 0.0).then_inc(ident_cleared, 1)
            pool.wait_ge(ident_cleared, 1)
            pool.affine_select(out=ident[:, :], in_=ident[:, :], compare_op=ALU.not_equal, fill=1.0, base=0,
                               pattern=[[-1, P]], channel_multiplier=1).then_inc(consts_set, 1)
            pool.memset(ones[:, :], 1.0).then_inc(consts_set, 1)

            def load_adj(ib, q):
                for a in range(QUAD):
                    dst = raw[q][a * B32:(a + 1) * B32, :].rearrange("p (g n) -> p g n", g=G32)
                    pool.dma_start(dst, adj_v[ib, a, :, :, q * QN:(q + 1) * QN]).then_inc(adj_loaded[q], 16)

            load_adj(0, 0)
            pool.wait_ge(gh_ready, TILES)
            pool.wait_ge(gl_ready, TILES)
            pool.wait_ge(mean_sum, 1)
            for q in range(1, QTR):
                load_adj(0, q)
            with pool.Fori(1, BLOCKS) as ib:
                for q in range(QTR):
                    pool.wait_ge(transposed, ib * UNITS + (2 * (q + 1) - UNITS))
                    load_adj(ib, q)

        @block.scalar
        def _(act):
            with act.Fori(0, CHUNKS) as c:
                act.wait_ge(var_ready, c + 1)
                act.activation(c16[:, 5, :], c16[:, 4, :], ACT.Sqrt).then_inc(sd_ready, 1)
                act.wait_ge(stats_ready, c + 1)

                def h_tiles(k):
                    n = c * CP + k
                    if k < 2:
                        act.wait_ge(z_multiplied, c * CP)
                        act.wait_ge(h_squared, c * CP)
                        act.wait_ge(a_step, c * CP)
                    else:
                        act.wait_ge(h_transposed, n - 1)
                        act.wait_ge(h_squared, n - 1)
                        act.wait_ge(a_step, n - 1)
                    for e in range(2):
                        t = c * CT + (2 * k + e)
                        act.activation(hb[k % 2][:, e, :], xz_t[:, bass.ds(t, 1), :], ACT.Relu,
                                       bias=nbias[:, bass.ds(t, 1)], scale=rstd[:, bass.ds(t, 1)]).then_inc(h_ready, 1)

                def h_square(k):
                    t = c * CT + 2 * k
                    act.wait_ge(h_ready, 2 * (c * CP + k) + 1)
                    act.wait_ge(a_step, c * CP + k)
                    act.activation(junk_a[:, 0:D - 1], hb[k % 2][:, 0, 1:D], ACT.Square,
                                   accum_out=ny2[:, bass.ds(t, 1)]).then_inc(a_step, 1)

                def hT_copy(k):
                    n = c * CP + k
                    act.wait_ge(h_transposed, n + 1)
                    act.wait_ge(z_multiplied, n - 1 if k >= 2 else c * CP)
                    act.activation(hT[k % 2], hTp[k % 2][:, :].rearrange("p (h e j) -> p h e j", h=DH, e=2),
                                   ACT.Copy).then_inc(hT_copied, 1)

                h_tiles(0)
                for k in range(CP):
                    if k + 1 < CP:
                        h_tiles(k + 1)
                    h_square(k)
                    hT_copy(k)

            act.wait_ge(node_v, 1)
            act.activation(tmp64, tmp64, ACT.Sqrt).then_inc(node_a, 1)
            act.activation(ny2, ny2, ACT.Sqrt).then_inc(node_a, 1)
            act.activation(n_, n2, ACT.Sqrt).then_inc(node_a, 1)
            act.wait_ge(node_v, 2)
            act.activation(c_, c_, ACT.Ln).then_inc(node_a, 1)
            act.wait_ge(node_v, 5)
            act.activation(w_, tv, ACT.Exp, bias=sc[:, 4:5]).then_inc(node_a, 1)
            act.wait_ge(w_ready, 1)
            with act.Fori(0, TILES) as t:
                act.activation(g[:, bass.ds(t, 1), 0, 1:D], xz_t[:, bass.ds(t, 1), 0:D - 1], ACT.Copy,
                               scale=gr[:, bass.ds(t, 1)]).then_inc(gh_ready, 1)

            def scale_unit(ib, u):
                n = ib * UNITS + u
                act.wait_ge(transposed, n + 1)
                if not (isinstance(ib, int) and ib == 0 and u < 2):
                    act.wait_ge(multiplied, (n - 1) * UT)
                mv = mT[u % 2][:, :, :, :].bitcast(BF16)
                for j in range(UT):
                    src = mv[:, j // 2, :, :].rearrange("p g (i e) -> p (g i) e", e=2)[:, :, j % 2]
                    act.activation(ms[:, (u % 2) * UT + j, :], src, ACT.Copy,
                                   scale=beta[:, u * UT + j:u * UT + j + 1]).then_inc(scaled, 1)

            def exp_rows(j, b):
                for k in range(RT):
                    act.wait_ge(neg_ready, j * RT + (k + 1))
                    act.activation(erow[b][:, k, :], erow[b][:, k, :], ACT.Exp).then_inc(exp_ready, 1)

            def square_rows(j, b):
                for k in range(RT):
                    act.wait_ge(elu_ready, j * RT + (k + 1))
                    act.wait_ge(elu_squared, j * RT + k)
                    act.activation(junk_a[:, 0:D - 1], hrow[:, k, 1:D], ACT.Square,
                                   accum_out=e8[:, 0, k:k + 1]).then_inc(elu_squared, 1)

            def ln_rows(j, b):
                act.wait_ge(ln_arg, j + 1)
                act.activation(e8[:, 5, 0:RT], e8[:, 5, 0:RT], ACT.Ln).then_inc(ln_ready, 1)

            def tanh_rows(j, b):
                act.wait_ge(scale_ready, j + 1)
                for k in range(RT):
                    act.activation(erow[b][:, k, :], hrow[:, k, :], ACT.Tanh,
                                   scale=e8[:, 6, k:k + 1]).then_inc(tanh_ready, 1)

            def cosh_rows(j, b):
                act.wait_ge(norm_ready, j + 1)
                act.activation(e8[:, 10, 0:RT], e8[:, 8, 0:RT], ACT.Exp).then_inc(cosh_ready, 1)

            early = {5: exp_rows, 7: square_rows}
            late = {2: ln_rows, 3: tanh_rows, 5: cosh_rows}

            def main(ib, b, prev, prev2):
                for u in range(UNITS):
                    scale_unit(ib, u)
                    if prev2 and u in late:
                        late[u](ib - 2, b)
                    if prev and u in early:
                        early[u](ib - 1, 1 - b)

            main(0, 0, False, False)
            main(1, 1, True, False)
            with act.Fori(0, BLOCKS // 2 - 1) as k:
                for b in range(2):
                    main(2 * k + 2 + b, b, True, True)
            for j, fs in ((BLOCKS - 2, late), (BLOCKS - 1, early), (BLOCKS - 1, late)):
                for f in fs.values():
                    f(j, j % 2)

        @block.tensor
        def _(pe):
            pe.wait_ge(consts_set, 6)
            pe.wait_ge(prep_ready, 1)
            for h in range(DH):
                pe.matmul(pm[:, h * P:(h + 1) * P], ones[:, :], diag[:, h, :], start=True, stop=True)\
                  .then_inc(prep_multiplied, 1)
            pe.wait_ge(prep_ready, 2)
            with pe.Fori(0, CHUNKS) as c:
                def turn(k):
                    n = c * CP + k
                    pe.wait_ge(h_ready, 2 * n + 2)
                    if k >= 2:
                        pe.wait_ge(hT_copied, n - 1)
                    else:
                        pe.wait_ge(hT_copied, c * CP)
                    for h in range(DH):
                        for e in range(2):
                            i = pe.transpose(hTp[k % 2][:, (h * 2 + e) * P:(h * 2 + e + 1) * P],
                                             hb[k % 2][:, e, h * P:(h + 1) * P], ident[:, :])
                    i.then_inc(h_transposed, 1)

                def mult(k):
                    n = c * CP + k
                    pe.wait_ge(hT_copied, n + 1)
                    if k >= 2:
                        pe.wait_ge(z_copied, n - 1)
                    else:
                        pe.wait_ge(z_copied, c * CP)
                    for e in range(2):
                        for h in range(DH):
                            i = pe.matmul(zp[k % 2][:, e * D:(e + 1) * D], hT[k % 2][:, h, e, :], wg[:, h, :],
                                          start=(h == 0), stop=(h == DH - 1))
                    i.then_inc(z_multiplied, 1)

                turn(0)
                for k in range(1, CP):
                    turn(k)
                    mult(k - 1)
                mult(CP - 1)
            pe.wait_ge(r_ready, 1)
            for h in range(DH):
                M = P if h == 0 else P - 1
                for t in range(TILES):
                    i = pe.matmul(pm[0:M, 2 * D - 2 + h:2 * D - 1 + h], xz_t[:, t, h * P:h * P + M], r_[:, t:t + 1],
                                  start=(t == 0), stop=(t == TILES - 1))
            i.then_inc(mean_sum, 1)
            pe.wait_ge(node_v, 3)
            pe.transpose(pm2[0:2, 0:P], sc[:, 0:2], ident[:, :]).then_inc(node_p, 1)
            pe.wait_ge(node_v, 4)
            pe.matmul(pm2[:, P:P + 2], ones[0:2, :], sc[0:2, 6:8], start=True, stop=True).then_inc(node_p, 1)
            pe.wait_ge(node_v, 6)
            for h in range(DH):
                K = P if h == 0 else P - 1
                i = pe.matmul(pm2[:, D:2 * D], diag[0:K, h, :], was[0:K, h, :], start=(h == 0), stop=(h == DH - 1))
            i.then_inc(node_p, 1)

            def multiply(ib, b, u, first):
                for j in range(UT):
                    t = u * UT + j
                    if first:
                        pe.wait_ge(gl_ready, t + 1)
                    pe.wait_ge(scaled, ib * TILES + (t + 1))
                    for h in range(DH):
                        for part in range(2):
                            i = pe.matmul(acc[b][h][:, :], g[:, t, part, h * P:(h + 1) * P], ms[:, t % SLOTS, :],
                                          start=(t == 0 and part == 0), stop=(t == TILES - 1 and part == 1))
                    i.then_inc(multiplied, 1)

            def project(j, ks):
                pe.wait_ge(acc_copied, (j + 1) * DH)
                for k in ks:
                    if not (isinstance(j, int) and j == 0 and k < 2):
                        pe.wait_ge(hp_read, j * RT + (k - 1))
                    for h in range(DH):
                        i = pe.matmul(hp[k % 2][:, 0:D + 1], uT[:, h, k * P:(k + 1) * P], wa[:, h, :],
                                      start=(h == 0), stop=(h == DH - 1))
                    i.then_inc(projected, 1)

            def main(ib, b, prev):
                for u in range(UNITS):
                    if u == 0 and not (isinstance(ib, int) and ib < 2):
                        pe.wait_ge(acc_copied, (ib - 1) * DH)
                    multiply(ib, b, u, isinstance(ib, int) and ib == 0)
                    if prev and u == 1:
                        project(ib - 1, (0, 1))
                    if prev and u == 3:
                        project(ib - 1, (2, 3))

            pe.wait_ge(g0_ready, 1)
            main(0, 0, False)
            main(1, 1, True)
            with pe.Fori(0, BLOCKS // 2 - 1) as k:
                for b in range(2):
                    main(2 * k + 2 + b, b, True)
            project(BLOCKS - 1, range(RT))

        @block.vector
        def _(dve):
            step = Chain(dve, v_step, 0)
            dve.memset(wg[:, :, :], 0.0).then_inc(consts_set, 1)
            dve.memset(was[:, :, :], 0.0).then_inc(consts_set, 1)
            step(dve.memset(wa[:, :, :], 0.0))
            dve.memset(wa[0:1, 0, D:D + 1], 1.0).then_inc(consts_set, 2)
            dve.wait_ge(weights_loaded, 16 * 7)
            for h in range(DH):
                step(dve.scalar_tensor_tensor(out=junk_v[:, :], in0=was[:, h, :], scalar=1.0, in1=a2b[:, :],
                                              op0=ALU.mult, op1=ALU.mult, accum_out=sc[:, 8 + h:9 + h]))
            dve.wait_ge(consts_set, 6)
            step(dve.tensor_scalar(diag[:, 0, :], ident[:, :], sc[:, 8:9], None, ALU.mult))
            dve.tensor_scalar(diag[:, 1, :], ident[:, :], sc[:, 9:10], None, ALU.mult).then_inc(prep_ready, 1)
            dve.wait_ge(prep_multiplied, DH)
            step(dve.tensor_copy(ub[:, :], pm[:, 0:D]))
            step(dve.scalar_tensor_tensor(out=junk_v[:, 0:D - 1], in0=wg[:, 0, 0:D - 1], scalar=1.0,
                                          in1=ub[:, 0:D - 1], op0=ALU.mult, op1=ALU.mult,
                                          accum_out=wg[:, 0, D - 1:D]))
            dve.scalar_tensor_tensor(out=junk_v[:, 0:D - 1], in0=wg[:, 1, 0:D - 1], scalar=1.0,
                                     in1=ub[:, 0:D - 1], op0=ALU.mult, op1=ALU.mult,
                                     accum_out=wg[:, 1, D - 1:D]).then_inc(prep_ready, 1)

            with dve.Fori(0, CHUNKS) as c:
                own = Chain(dve, v_chunk, c * VCH)
                cols = bass.ts(c, CT)
                dve.wait_ge(x_loaded, (c + 1) * (16 * QUAD))
                for t in range(CT):
                    i = dve.bn_stats(st[:, t, :], xz_t[:, bass.ds(c * CT + t, 1), :])
                own(i)
                s, d, cv, v, ve, sd = [c16[:, i, :] for i in range(6)]
                dve.tensor_tensor(s, st[:, :, 1], st[:, :, 4], ALU.add)
                dve.tensor_tensor(d, st[:, :, 1], st[:, :, 4], ALU.subtract)
                own(dve.tensor_tensor(cv, st[:, :, 2], st[:, :, 5], ALU.add))
                own(dve.scalar_tensor_tensor(out=v, in0=d, scalar=0.25, in1=d, op0=ALU.mult, op1=ALU.mult))
                own(dve.scalar_tensor_tensor(out=v, in0=cv, scalar=1.0 / D, in1=v, op0=ALU.mult, op1=ALU.add))
                dve.tensor_scalar(ve, v, LN_EPS, None, ALU.add).then_inc(var_ready, 1)
                dve.wait_ge(sd_ready, c + 1)
                own(dve.reciprocal(rstd[:, cols], sd))
                own(dve.scalar_tensor_tensor(out=nbias[:, cols], in0=s, scalar=-0.5, in1=rstd[:, cols],
                                             op0=ALU.mult, op1=ALU.mult))
                own(dve.tensor_tensor(q0[:, cols], xz_t[:, cols, 0], rstd[:, cols], ALU.mult))
                own(dve.tensor_tensor(q0[:, cols], q0[:, cols], nbias[:, cols], ALU.add))
                dve.tensor_scalar(q0[:, cols], q0[:, cols], THETA_MIN, None, ALU.max).then_inc(stats_ready, 1)
                assert own.n == VCH

                def z_square(k):
                    t = c * CT + 2 * k
                    dve.wait_ge(z_multiplied, c * CP + (k + 1))
                    dve.tensor_scalar(xz_t[:, bass.ds(t, 2), :], zp[k % 2][:, :].rearrange("p (t d) -> p t d", d=D),
                                      1.0, None, ALU.mult).then_inc(z_copied, 1)
                    dve.wait_ge(z_copied, c * CP + (k + 1))
                    for e in range(2):
                        t = c * CT + (2 * k + e)
                        dve.wait_ge(z_squared, 2 * (c * CP + k) + e)
                        dve.scalar_tensor_tensor(out=junk_v[:, 0:D - 1], in0=xz_t[:, bass.ds(t, 1), 0:D - 1],
                                                     scalar=1.0, in1=xz_t[:, bass.ds(t, 1), 0:D - 1],
                                                     op0=ALU.mult, op1=ALU.mult, accum_out=n2[:, bass.ds(t, 1)])\
                           .then_inc(z_squared, 1)

                for k in range(CP):
                    t = c * CT + (2 * k + 1)
                    dve.wait_ge(h_ready, 2 * (c * CP + k) + 2)
                    dve.wait_ge(h_squared, c * CP + k)
                    dve.scalar_tensor_tensor(out=junk_h[:, 0:D - 1], in0=hb[k % 2][:, 1, 1:D], scalar=1.0,
                                             in1=hb[k % 2][:, 1, 1:D], op0=ALU.mult, op1=ALU.mult,
                                             accum_out=ny2[:, bass.ds(t, 1)]).then_inc(h_squared, 1)
                    if k >= 1:
                        z_square(k - 1)
                z_square(CP - 1)

            dve.wait_ge(z_squared, TILES)
            dve.wait_ge(a_step, TILES // 2)
            dve.wait_ge(stats_ready, CHUNKS)
            step(dve.tensor_scalar(tmp65, q0, 1.0, None, ALU.subtract))
            step(dve.scalar_tensor_tensor(out=tmp64, in0=q0, scalar=1.0, in1=tmp65, op0=ALU.add, op1=ALU.mult))
            step(dve.tensor_scalar(ny2, ny2, NORM_FLOOR2, None, ALU.max))
            dve.tensor_scalar(n2, n2, NORM_FLOOR2, None, ALU.max).then_inc(node_v, 1)
            dve.wait_ge(node_a, 3)
            dve.tensor_tensor(c_, q0, tmp64, ALU.add).then_inc(node_v, 1)
            step(dve.reciprocal(tmp65, ny2))
            step(dve.reciprocal(tmp64, n_))
            dve.wait_ge(node_a, 4)
            step(dve.scalar_tensor_tensor(out=c_, in0=c_, scalar=ACOSH_MIN, in1=tmp65, op0=ALU.max, op1=ALU.mult))
            step(dve.tensor_tensor(a_, c_, n_, ALU.mult))
            step(dve.tensor_scalar(a_, a_, ACOSH_MIN, None, ALU.max))
            step(dve.tensor_tensor(r_, a_, tmp64, ALU.mult))
            dve.tensor_tensor(tv, r_, xz_t[:, :, D - 1], ALU.mult).then_inc(r_ready, 1)
            dve.wait_ge(r_ready, 1)
            step(dve.tensor_reduce(sc[:, 0:1], tv, AX.X, ALU.max))
            step(dve.tensor_reduce(sc[:, 1:2], tv, AX.X, ALU.min))
            dve.tensor_scalar(sc[:, 1:2], sc[:, 1:2], -1.0, None, ALU.mult).then_inc(node_v, 1)
            dve.wait_ge(node_p, 1)
            step(dve.tensor_reduce(sc[0:2, 2:3], pm2[0:2, 0:P], AX.X, ALU.max))
            dve.tensor_scalar(sc[0:2, 6:8], ident[0:2, 0:2], sc[0:2, 2:3], None, ALU.mult).then_inc(node_v, 1)
            dve.wait_ge(node_p, 2)
            dve.tensor_scalar(sc[:, 4:5], pm2[:, P:P + 1], -1.0, None, ALU.mult).then_inc(node_v, 1)
            dve.wait_ge(node_a, 5)
            step(dve.scalar_tensor_tensor(out=tmp64, in0=a_, scalar=1.0, in1=w_, op0=ALU.max, op1=ALU.mult))
            step(dve.tensor_scalar(tmp64.bitcast(I32), tmp64.bitcast(I32), EXP_MASK, None, ALU.bitwise_and))
            step(dve.tensor_scalar(beta, tmp64, BETA, None, ALU.mult))
            step(dve.reciprocal(tmp65, beta))
            step(dve.tensor_tensor(gs, w_, tmp65, ALU.mult))
            dve.tensor_tensor(gr, gs, r_, ALU.mult).then_inc(w_ready, 1)
            step(dve.tensor_copy(g[:, :, 0, 0], gs))
            dve.tensor_tensor(g[:, :, 1, 0], gs, g[:, :, 0, 0], ALU.subtract).then_inc(g0_ready, 1)
            dve.wait_ge(w_ready, 1)
            with dve.Fori(0, TILES) as t:
                dve.wait_ge(gh_ready, t + 1)
                dve.scalar_tensor_tensor(out=g[:, bass.ds(t, 1), 1, 1:D], in0=xz_t[:, bass.ds(t, 1), 0:D - 1],
                                         scalar=gr[:, bass.ds(t, 1)], in1=g[:, bass.ds(t, 1), 0, 1:D],
                                         op0=ALU.mult, op1=ALU.subtract).then_inc(gl_ready, 1)
            dve.wait_ge(mean_sum, 1)
            step(dve.tensor_copy(sc[:, 10:11], pm[:, 2 * D - 2:2 * D - 1]))
            step(dve.tensor_copy(sc[0:P - 1, 11:12], pm[0:P - 1, 2 * D - 1:2 * D]))
            step(dve.tensor_scalar(diag[:, 0, :], ones[:, :], sc[:, 10:11], 1.0 / N, ALU.mult, ALU.mult))
            dve.tensor_scalar(diag[0:P - 1, 1, :], ones[0:P - 1, :], sc[0:P - 1, 11:12], 1.0 / N, ALU.mult, ALU.mult)\
               .then_inc(node_v, 1)
            dve.wait_ge(node_p, 3)
            step(dve.tensor_copy(hmean[:, :], pm2[:, D:2 * D]))

            def turn_unit(ib, u):
                n = ib * UNITS + u
                q = u // 2
                if u % 2 == 0:
                    dve.wait_ge(adj_loaded[q], (ib + 1) * (16 * QUAD))
                    dve.tensor_scalar(raw[q], raw[q], 0.0, None, ALU.is_gt).then_inc(is_set, 1)
                    dve.wait_ge(is_set, ib * QTR + (q + 1))
                if not (isinstance(ib, int) and ib == 0 and u < 2):
                    dve.wait_ge(scaled, (n - 1) * UT)
                src = raw[q].bitcast(U32).rearrange("p (g h m w) -> p h m g w", h=2, m=UM, w=B32)
                dve.transpose(mT[u % 2][:, :, :, :], src[:, u % 2]).then_inc(transposed, 1)

            def root(own, dst, arg, half):
                dve.tensor_scalar(dst.bitcast(I32), arg.bitcast(I32), 0.5, SQRT_MAGIC, ALU.mult, ALU.add)
                own(dve.tensor_scalar(half, arg, 0.5, None, ALU.mult))
                rec = e8[:, 15, 0:dst.shape[1]]
                for _ in range(3):
                    own(dve.reciprocal(rec, dst))
                    own(dve.tensor_tensor(rec, rec, half, ALU.mult))
                    own(dve.scalar_tensor_tensor(out=dst, in0=dst, scalar=0.5, in1=rec, op0=ALU.mult, op1=ALU.add))

            def copy_acc(j, b):
                dve.wait_ge(multiplied, (j + 1) * TILES)
                dve.wait_ge(projected, j * RT)
                for h in range(DH):
                    dve.tensor_copy(uT[:, h, :], acc[b][h][:, :]).then_inc(acc_copied, 1)

            def normalise(j, b, ks):
                own = Chain(dve, v_norm, j * N_NORM + 4 * ks[0])
                for k in ks:
                    dve.wait_ge(projected, j * RT + (k + 1))
                    dve.wait_ge(tanh_ready, j * RT)
                    empty, den, rden = [e8[:, i, k:k + 1] for i in (1, 2, 3)]
                    own(dve.tensor_scalar(empty, hp[k % 2][:, D:D + 1], 0.0, None, ALU.is_equal))
                    own(dve.tensor_tensor(den, hp[k % 2][:, D:D + 1], empty, ALU.add))
                    own(dve.reciprocal(rden, den))
                    dve.scalar_tensor_tensor(out=hrow[:, k, :], in0=hmean[:, :], scalar=empty,
                                             in1=hp[k % 2][:, 0:D], op0=ALU.mult, op1=ALU.add).then_inc(hp_read, 1)
                    dve.wait_ge(hp_read, j * RT + (k + 1))
                    dve.tensor_scalar(erow[b][:, k, :], hrow[:, k, :], rden, 0.0, ALU.mult, ALU.min)\
                       .then_inc(neg_ready, 1)
                    own(dve.tensor_scalar(hrow[:, k, :], hrow[:, k, :], rden, 0.0, ALU.mult, ALU.max))
                assert own.n == 4 * len(ks)

            def elu(j, b):
                for k in range(RT):
                    dve.wait_ge(exp_ready, j * RT + (k + 1))
                    dve.scalar_tensor_tensor(out=hrow[:, k, :], in0=erow[b][:, k, :], scalar=-1.0, in1=hrow[:, k, :],
                                             op0=ALU.add, op1=ALU.add).then_inc(elu_ready, 1)

            def elu_norm(j):
                own = Chain(dve, v_root, j * N_ROOT)
                dve.wait_ge(elu_squared, (j + 1) * RT)
                own(dve.tensor_scalar(e8[:, 4, 0:RT], e8[:, 0, 0:RT], NORM_FLOOR2, None, ALU.max))
                own(dve.tensor_scalar(e8[:, 4, RT:2 * RT], e8[:, 0, 0:RT], 1.0, None, ALU.add))
                root(own, e8[:, 7, :], e8[:, 4, :], e8[:, 11, :])
                dve.tensor_tensor(e8[:, 5, 0:RT], e8[:, 7, 0:RT], e8[:, 7, RT:2 * RT], ALU.add).then_inc(ln_arg, 1)
                assert own.n == N_ROOT

            def tanh_scale(j):
                own = Chain(dve, v_scale, j * N_SCALE)
                own(dve.reciprocal(e8[:, 11, 0:RT], e8[:, 7, 0:RT]))
                own(dve.tensor_scalar(e8[:, 11, 0:RT], e8[:, 11, 0:RT], 0.5, None, ALU.mult))
                dve.wait_ge(ln_ready, j + 1)
                dve.scalar_tensor_tensor(out=e8[:, 6, 0:RT], in0=e8[:, 5, 0:RT], scalar=ACOSH_MIN,
                                         in1=e8[:, 11, 0:RT], op0=ALU.max, op1=ALU.mult).then_inc(scale_ready, 1)
                assert own.n == N_SCALE

            def sigmoid(j, b):
                own = Chain(dve, v_sig, j * N_SIG)
                for k in range(RT):
                    dve.wait_ge(tanh_ready, j * RT + (k + 1))
                    own(dve.tensor_scalar(erow[b][:, k, :], erow[b][:, k, :], 0.5, 0.5, ALU.mult, ALU.add))
                    own(dve.scalar_tensor_tensor(out=junk_v[:, 0:D - 1], in0=erow[b][:, k, 1:D], scalar=1.0,
                                                 in1=erow[b][:, k, 1:D], op0=ALU.mult, op1=ALU.mult,
                                                 accum_out=e8[:, 9, k:k + 1]))
                own(dve.tensor_scalar(e8[:, 9, 0:RT], e8[:, 9, 0:RT], NORM_FLOOR2, None, ALU.max))
                root(own, e8[:, 8, 0:RT], e8[:, 9, 0:RT], e8[:, 14, 0:RT])
                dve.reciprocal(e8[:, 14, 0:RT], e8[:, 8, 0:RT]).then_inc(norm_ready, 1)
                assert own.n == N_SIG

            def finish(j, pair, b):
                own = Chain(dve, v_fin, j * N_FIN)
                dve.wait_ge(norm_ready, j + 1)
                dve.wait_ge(cosh_ready, j + 1)
                dve.wait_ge(xt_loaded[b], (pair + 1) * 16)
                ex, inv, sh, ch, rn = [e8[:, i, 0:RT] for i in (10, 11, 12, 13, 14)]
                own(dve.reciprocal(inv, ex))
                own(dve.tensor_tensor(sh, ex, inv, ALU.subtract))
                own(dve.tensor_tensor(ch, ex, inv, ALU.add))
                own(dve.scalar_tensor_tensor(out=sh, in0=sh, scalar=0.5, in1=rn, op0=ALU.mult, op1=ALU.mult))
                for k in range(RT):
                    dve.scalar_tensor_tensor(out=xt[b][:, k, 1:D], in0=erow[b][:, k, 1:D], scalar=sh[:, k:k + 1],
                                             in1=xt[b][:, k, 1:D], op0=ALU.mult, op1=ALU.add)
                dve.scalar_tensor_tensor(out=xt[b][:, :, 0], in0=ch, scalar=0.5, in1=xt[b][:, :, 0],
                                         op0=ALU.mult, op1=ALU.add).then_inc(rows_ready, 1)
                assert own.n == N_FIN

            def main(ib, pair, b, prev, prev2):
                for u in range(UNITS):
                    turn_unit(ib, u)
                    if prev2 and u == 1:
                        elu_norm(ib - 2)
                    if prev2 and u == 3:
                        tanh_scale(ib - 2)
                    if prev and u == 3:
                        copy_acc(ib - 1, 1 - b)
                    if prev and u == 4:
                        normalise(ib - 1, 1 - b, (0, 1))
                    if prev2 and u == 5:
                        sigmoid(ib - 2, b)
                    if prev and u == 6:
                        normalise(ib - 1, 1 - b, (2, 3))
                    if prev and u == 7:
                        elu(ib - 1, 1 - b)
                    if prev2 and u == 7:
                        finish(ib - 2, pair - 1, b)

            main(0, 0, 0, False, False)
            main(1, 0, 1, True, False)
            with dve.Fori(0, BLOCKS // 2 - 1) as k:
                for b in range(2):
                    main(2 * k + 2 + b, k + 1, b, True, True)
            j = BLOCKS - 2
            elu_norm(j)
            tanh_scale(j)
            sigmoid(j, 0)
            finish(j, j // 2, 0)
            j = BLOCKS - 1
            copy_acc(j, 1)
            normalise(j, 1, (0, 1))
            normalise(j, 1, (2, 3))
            elu(j, 1)
            elu_norm(j)
            tanh_scale(j)
            sigmoid(j, 1)
            finish(j, j // 2, 1)


_INS = ["x", "adj", "L0_gnn_W_gcn", "L0_gnn_W_att", "L0_gnn_a_att"]


def kernel(**inputs):
    import numpy as _np
    import concourse.bacc as _bacc
    from concourse import mybir as _mybir
    from concourse.bass_utils import run_bass_kernel_spmd as _run

    nc = _bacc.Bacc("TRN2", target_bir_lowering=False, num_devices=1)
    arrays, args = {}, []
    for name in _INS:
        a = _np.ascontiguousarray(inputs[name])
        arrays[f"in_{name}"] = a
        args.append(nc.dram_tensor(f"in_{name}", a.shape, _mybir.dt.from_np(a.dtype), kind="ExternalInput").ap())
    args.append(nc.dram_tensor("out_rows", inputs["x"].shape, _mybir.dt.float32, kind="ExternalOutput").ap())
    gnn_kernel(nc, *args)
    r = _run(nc, [arrays], core_ids=[0])
    return r.results[0]["out_rows"]
```

```python
import math
from contextlib import ExitStack

import concourse.bass as bass
from concourse import mybir


ALU = mybir.AluOpType
ACT = mybir.ActivationFunctionType
AX = mybir.AxisListType
F32 = mybir.dt.float32
BF16 = mybir.dt.bfloat16
F16 = mybir.dt.float16
U32 = mybir.dt.uint32
I32 = mybir.dt.int32

P = 128
QUAD = 4
B32 = P // QUAD
LN_EPS = 1e-5
NORM_FLOOR2 = 1e-30
THETA_MIN = 1.0 + 2.0 ** -23
ACOSH_MIN = math.acosh(THETA_MIN)
EXP_MASK = 0x7F800000
BETA = 2.0 ** -14
SQRT_MAGIC = float(0x1FBD1DF5)


def after(eng, sem, value):
    if not (isinstance(value, int) and value <= 0):
        eng.wait_ge(sem, value)


class Chain:

    def __init__(self, eng, sem, base):
        self.eng, self.sem, self.base, self.n = eng, sem, base, 0

    def __call__(self, ins):
        ins.then_inc(self.sem, 1)
        self.n += 1
        self.eng.wait_ge(self.sem, self.base + self.n)


def gnn_kernel(nc, x, adj, w_gcn, w_att, a_att, out):
    N, D = x.shape
    DH = D // P
    NQ = N // QUAD
    TILES = N // P
    PAIRS = TILES // 2
    CHUNKS = 8
    CT = TILES // CHUNKS
    CP = CT // 2
    IB = 512
    BLOCKS = N // IB
    G32 = IB // B32
    QTR = 4
    QN = NQ // QTR
    UNITS = 2 * QTR
    UT = TILES // UNITS
    UM = UT // 2
    SLOTS = 2 * UT
    RT = IB // P

    with ExitStack() as ctx:
        def sb(name, shape, dt):
            return ctx.enter_context(nc.sbuf_tensor(name, shape, dt))

        def pb(name, shape, dt=F32):
            return ctx.enter_context(nc.psum_tensor(name, shape, dt))

        def sem(name):
            return ctx.enter_context(nc.semaphore(name))

        xz = sb("xz", [P, TILES * D], F32)
        xz_t = xz[:, :].rearrange("p (t d) -> p t d", d=D)
        LOADF = G32 * QN // 2
        NRAW = 2
        raw = [sb(f"raw{i}", [P, G32 * QN], BF16)[:, :] for i in range(NRAW)]
        raw += [xz[:, i * LOADF:(i + 1) * LOADF].bitcast(BF16) for i in range(QTR - NRAW)]
        rest = (QTR - NRAW) * LOADF

        def row_buffer(i):
            return xz[:, rest + i * RT * D:rest + (i + 1) * RT * D]

        uT = row_buffer(0).rearrange("p (h i) -> p h i", h=DH)
        hrow, *erow = [row_buffer(i).rearrange("p (k d) -> p k d", d=D) for i in (1, 2, 3)]
        xt = [row_buffer(i).rearrange("p (k d) -> p k d", d=D) for i in (4, 5)]
        gbuf = sb("gbuf", [P, TILES * 2 * D], F16)
        g = gbuf[:, :].rearrange("p (t s d) -> p t s d", s=2, d=D)
        ring = gbuf[:, 0:4 * 4 * D * 2].bitcast(F32)
        hb = [ring[:, i * 2 * D:(i + 1) * 2 * D].rearrange("p (e d) -> p e d", e=2) for i in range(2)]
        hT = [ring[:, (2 + i) * 2 * D:(3 + i) * 2 * D].rearrange("p (h e j) -> p h e j", h=DH, e=2) for i in range(2)]
        prep = gbuf[:, 4 * 4 * D * 2:4 * 4 * D * 2 + 4 * D].bitcast(F32)
        a2b, ub = prep[:, 0:D], prep[:, D:2 * D]
        mT = [sb(f"mT{i}", [P, UM, G32, B32], U32) for i in range(2)]
        ms = sb("ms", [P, SLOTS, IB], BF16)
        wg = sb("wg", [P, DH, D], F32)
        wa = sb("wa", [P, DH, D + 1], F32)
        cf = sb("cf", [P, TILES, 3], BF16)
        ident = sb("ident", [P, P], F32)
        ones = sb("ones", [P, P], F32)
        diag = sb("diag", [P, DH, P], F32)
        hmean = sb("hmean", [P, D], F32)
        junk_v = sb("junk_v", [P, D], F32)
        junk_a = sb("junk_a", [P, D], F32)
        st = sb("st", [P, CT, 6], F32)
        c16 = sb("c16", [P, 8, CT], F32)
        s64 = sb("s64", [P, 16, TILES], F32)
        (rstd, nbias, q0, ny2, n2, c_, n_, a_, r_, w_, beta, gs, gr, tv, tmp64, tmp65) = [s64[:, i, :] for i in range(16)]
        sc = sb("sc", [P, 16], F32)
        e8 = sb("e8", [P, 16, 8], F32)

        acc = [[pb(f"acc{b}{h}", [P, IB]) for h in range(DH)] for b in range(2)]
        hp = [pb(f"hp{i}", [P, 512]) for i in range(2)]
        pm = pb("pm", [P, 512])
        pm2 = pb("pm2", [P, 512])
        hTp = [acc[0][i] for i in range(2)]
        zp = [acc[1][i] for i in range(2)]

        consts_set = sem("consts_set")
        ident_cleared = sem("ident_cleared")
        weights_loaded = sem("weights_loaded")
        x_loaded = [sem(f"x_loaded{c}") for c in range(CHUNKS)]
        prep_ready = sem("prep_ready")
        prep_multiplied = sem("prep_multiplied")
        var_ready = sem("var_ready")
        sd_ready = sem("sd_ready")
        stats_ready = sem("stats_ready")
        h_ready = sem("h_ready")
        h_transposed = sem("h_transposed")
        hT_copied = sem("hT_copied")
        z_multiplied = sem("z_multiplied")
        z_copied = sem("z_copied")
        z_squared = sem("z_squared")
        v_step = sem("v_step")
        r_ready = sem("r_ready")
        v_chunk = sem("v_chunk")
        v_norm = sem("v_norm")
        v_root = sem("v_root")
        v_scale = sem("v_scale")
        v_sig = sem("v_sig")
        v_fin = sem("v_fin")
        a_step = sem("a_step")
        node_v = sem("node_v")
        node_a = sem("node_a")
        node_p = sem("node_p")
        w_ready = sem("w_ready")
        node_sum = sem("node_sum")
        split_high = sem("split_high")
        split = sem("split")
        g0_ready = sem("g0_ready")
        adj_loaded = [sem(f"adj_loaded{i}") for i in range(QTR)]
        is_set = sem("is_set")
        transposed = sem("transposed")
        scaled = sem("scaled")
        multiplied = sem("multiplied")
        acc_copied = sem("acc_copied")
        projected = sem("projected")
        hp_read = sem("hp_read")
        neg_ready = sem("neg_ready")
        exp_ready = sem("exp_ready")
        elu_ready = sem("elu_ready")
        elu_squared = sem("elu_squared")
        ln_arg = sem("ln_arg")
        ln_ready = sem("ln_ready")
        scale_ready = sem("scale_ready")
        tanh_ready = sem("tanh_ready")
        norm_ready = sem("norm_ready")
        cosh_ready = sem("cosh_ready")
        rows_ready = sem("rows_ready")
        xt_loaded = [sem(f"xt_loaded{i}") for i in range(2)]
        stored = [sem(f"stored{i}") for i in range(2)]

        x_nodes = x.rearrange("(a m w e) d -> a w m (e d)", a=QUAD, w=B32, e=2)
        x_rows = x.rearrange("(b k p) d -> b p k d", k=RT, p=P)
        out_rows = out.rearrange("(b k p) d -> b p k d", k=RT, p=P)
        adj_v = adj.rearrange("(b g i) (a n) -> b a i g n", g=G32, i=B32, a=QUAD)
        VCH = 10
        N_NORM, N_ROOT, N_SCALE, N_SIG, N_FIN = 16, 12, 2, 2 * 4 + 11, 4

        block = ctx.enter_context(nc.Block())

        @block.sync
        def _(sp):
            def load_x(c):
                for a in range(QUAD):
                    dst = xz_t[a * B32:(a + 1) * B32, bass.ts(c, CT), :]
                    sp.dma_start(dst.rearrange("p (m e) d -> p m (e d)", e=2),
                                 x_nodes[a, :, bass.ts(c, CP), :]).then_inc(x_loaded[c], 16)

            load_x(0)
            sp.wait_ge(consts_set, 4)
            sp.dma_start(wg[1:P, 0, 0:D - 1], w_gcn[0:P - 1, :]).then_inc(weights_loaded, 16)
            sp.dma_start(wg[:, 1, 0:D - 1], w_gcn[P - 1:D - 1, :]).then_inc(weights_loaded, 16)
            sp.dma_start(wa[:, 0, 0:D], w_att[1:P + 1, :]).then_inc(weights_loaded, 16)
            sp.dma_start(wa[0:P - 1, 1, 0:D], w_att[P + 1:D, :]).then_inc(weights_loaded, 16)
            sp.dma_start(a2b[:, :], a_att[D:2 * D, :].rearrange("d o -> o d").to_broadcast([P, D])).then_inc(weights_loaded, 16)
            for c in range(1, CHUNKS):
                load_x(c)
            sp.wait_ge(split, TILES)

            def load_rows(j, b):
                sp.dma_start(xt[b][:, :, :], x_rows[j, :, :, :]).then_inc(xt_loaded[b], 16)

            def store_rows(j, b):
                sp.wait_ge(rows_ready, j + 1)
                sp.dma_start(out_rows[j, :, :, :], xt[b][:, :, :]).then_inc(stored[b], 16)

            load_rows(0, 0)
            load_rows(1, 1)
            with sp.Fori(0, BLOCKS // 2 - 1) as k:
                for b in range(2):
                    store_rows(2 * k + b, b)
                    sp.wait_ge(stored[b], 16 * (k + 1))
                    load_rows(2 * k + 2 + b, b)
            for b in range(2):
                store_rows(BLOCKS - 2 + b, b)
            for b in range(2):
                sp.wait_ge(stored[b], 16 * (BLOCKS // 2))

        @block.gpsimd
        def _(pool):
            pool.memset(ident[:, :], 0.0).then_inc(ident_cleared, 1)
            pool.wait_ge(ident_cleared, 1)
            pool.affine_select(out=ident[:, :], in_=ident[:, :], compare_op=ALU.not_equal, fill=1.0, base=0,
                               pattern=[[-1, P]], channel_multiplier=1).then_inc(consts_set, 1)
            pool.memset(ones[:, :], 1.0).then_inc(consts_set, 1)

            def load_adj(ib, q):
                for a in range(QUAD):
                    dst = raw[q][a * B32:(a + 1) * B32, :].rearrange("p (g n) -> p g n", g=G32)
                    pool.dma_start(dst, adj_v[ib, a, :, :, q * QN:(q + 1) * QN]).then_inc(adj_loaded[q], 16)

            for q in range(NRAW):
                load_adj(0, q)
            for q in range(NRAW):
                pool.wait_ge(adj_loaded[q], 16 * QUAD)
                pool.tensor_scalar(raw[q], raw[q], 0.0, None, ALU.is_gt).then_inc(is_set, 1)
            for q in range(NRAW, QTR):
                pool.wait_ge(split, (q - NRAW + 1) * (TILES // QTR))
                load_adj(0, q)
            with pool.Fori(1, BLOCKS) as ib:
                for q in range(QTR):
                    pool.wait_ge(transposed, ib * UNITS + (2 * (q + 1) - UNITS))
                    load_adj(ib, q)

        @block.scalar
        def _(act):
            def deviation(c):
                act.wait_ge(var_ready, c + 1)
                act.activation(c16[:, 5, :], c16[:, 4, :], ACT.Sqrt).then_inc(sd_ready, 1)

            def h_tiles(n, k):
                after(act, h_transposed, n - 1)
                after(act, a_step, 2 * (n - 1))
                for e in range(2):
                    t = 2 * n + e
                    act.activation(hb[k % 2][:, e, :], xz_t[:, t, :], ACT.Relu,
                                   bias=nbias[:, t:t + 1], scale=rstd[:, t:t + 1]).then_inc(h_ready, 1)

            def h_square(n, k):
                act.wait_ge(h_ready, 2 * n + 2)
                for t in (2 * n, 2 * n + 1):
                    after(act, a_step, t)
                    act.activation(junk_a[:, 0:D - 1], hb[k % 2][:, t % 2, 1:D], ACT.Square,
                                   accum_out=ny2[:, t:t + 1]).then_inc(a_step, 1)

            def hT_copy(n, k):
                act.wait_ge(h_transposed, n + 1)
                after(act, z_multiplied, n - 1)
                act.activation(hT[k % 2], hTp[k % 2][:, :].rearrange("p (h e j) -> p h e j", h=DH, e=2),
                               ACT.Copy).then_inc(hT_copied, 1)

            def node_chunk(c, last=False):
                for k in range(CP):
                    n = c * CP + k
                    if k == CP - 1 and not last:
                        deviation(c + 1)
                        act.wait_ge(stats_ready, c + 2)
                    if not (last and k == CP - 1):
                        h_tiles(n + 1, k + 1)
                    h_square(n, k)
                    hT_copy(n, k)

            deviation(0)
            act.wait_ge(stats_ready, 1)
            h_tiles(0, 0)
            for c in range(CHUNKS):
                node_chunk(c, last=(c == CHUNKS - 1))

            act.wait_ge(node_v, 1)
            act.activation(tmp64, tmp64, ACT.Sqrt).then_inc(node_a, 1)
            act.activation(ny2, ny2, ACT.Sqrt).then_inc(node_a, 1)
            act.activation(n_, n2, ACT.Sqrt).then_inc(node_a, 1)
            act.wait_ge(node_v, 2)
            act.activation(c_, c_, ACT.Ln).then_inc(node_a, 1)
            act.wait_ge(node_v, 5)
            act.activation(w_, tv, ACT.Exp, bias=sc[:, 4:5]).then_inc(node_a, 1)
            act.wait_ge(w_ready, 1)

            def scale_unit(ib, u):
                n = ib * UNITS + u
                act.wait_ge(transposed, n + 1)
                if not (isinstance(ib, int) and ib == 0 and u < 2):
                    act.wait_ge(multiplied, (n - 1) * UT)
                mv = mT[u % 2][:, :, :, :].bitcast(BF16)
                for j in range(UT):
                    src = mv[:, j // 2, :, :].rearrange("p g (i e) -> p (g i) e", e=2)[:, :, j % 2]
                    act.activation(ms[:, (u % 2) * UT + j, :], src, ACT.Copy,
                                   scale=beta[:, u * UT + j:u * UT + j + 1]).then_inc(scaled, 1)

            def exp_rows(j, b):
                for k in range(RT):
                    act.wait_ge(neg_ready, j * RT + (k + 1))
                    act.activation(erow[b][:, k, :], erow[b][:, k, :], ACT.Exp).then_inc(exp_ready, 1)

            def square_rows(j, b):
                for k in range(RT):
                    act.wait_ge(elu_ready, j * RT + (k + 1))
                    after(act, elu_squared, j * RT + k)
                    act.activation(junk_a[:, 0:D - 1], hrow[:, k, 1:D], ACT.Square,
                                   accum_out=e8[:, 0, k:k + 1]).then_inc(elu_squared, 1)

            def ln_rows(j, b):
                act.wait_ge(ln_arg, j + 1)
                act.activation(e8[:, 5, 0:RT], e8[:, 5, 0:RT], ACT.Ln).then_inc(ln_ready, 1)

            def tanh_rows(j, b):
                act.wait_ge(scale_ready, j + 1)
                for k in range(RT):
                    act.activation(erow[b][:, k, :], hrow[:, k, :], ACT.Tanh,
                                   scale=e8[:, 6, k:k + 1]).then_inc(tanh_ready, 1)

            def cosh_rows(j, b):
                act.wait_ge(norm_ready, j + 1)
                act.activation(e8[:, 10, 0:RT], e8[:, 8, 0:RT], ACT.Exp).then_inc(cosh_ready, 1)

            early = {5: exp_rows, 7: square_rows}
            late = {2: ln_rows, 3: tanh_rows, 5: cosh_rows}

            def main(ib, b, prev, prev2):
                for u in range(UNITS):
                    scale_unit(ib, u)
                    if prev2 and u in late:
                        late[u](ib - 2, b)
                    if prev and u in early:
                        early[u](ib - 1, 1 - b)

            main(0, 0, False, False)
            main(1, 1, True, False)
            with act.Fori(0, BLOCKS // 2 - 1) as k:
                for b in range(2):
                    main(2 * k + 2 + b, b, True, True)
            for j, fs in ((BLOCKS - 2, late), (BLOCKS - 1, early), (BLOCKS - 1, late)):
                for f in fs.values():
                    f(j, j % 2)

        @block.tensor
        def _(pe):
            pe.wait_ge(consts_set, 4)
            pe.wait_ge(prep_ready, 1)
            for h in range(DH):
                pe.matmul(pm[:, h * P:(h + 1) * P], ones[:, :], diag[:, h, :], start=True, stop=True)\
                  .then_inc(prep_multiplied, 1)

            def turn(n, k):
                pe.wait_ge(h_ready, 2 * n + 2)
                after(pe, hT_copied, n - 1)
                for h in range(DH):
                    for e in range(2):
                        i = pe.transpose(hTp[k % 2][:, (h * 2 + e) * P:(h * 2 + e + 1) * P],
                                         hb[k % 2][:, e, h * P:(h + 1) * P], ident[:, :])
                i.then_inc(h_transposed, 1)

            def mult(n, k):
                pe.wait_ge(hT_copied, n + 1)
                after(pe, z_copied, n - 1)
                for e in range(2):
                    for h in range(DH):
                        i = pe.matmul(zp[k % 2][:, e * D:(e + 1) * D], hT[k % 2][:, h, e, :], wg[:, h, :],
                                      start=(h == 0), stop=(h == DH - 1))
                i.then_inc(z_multiplied, 1)

            def node_chunk(c, last=False):
                for k in range(CP):
                    if not (last and k == CP - 1):
                        turn(c * CP + k + 1, k + 1)
                    mult(c * CP + k, k)

            turn(0, 0)
            pe.wait_ge(prep_ready, 2)
            for c in range(CHUNKS):
                node_chunk(c, last=(c == CHUNKS - 1))

            pe.wait_ge(node_v, 3)
            pe.transpose(pm2[0:2, 0:P], sc[:, 0:2], ident[:, :]).then_inc(node_p, 1)
            pe.wait_ge(node_v, 4)
            pe.matmul(pm2[:, P:P + 2], ones[0:2, :], sc[0:2, 6:8], start=True, stop=True).then_inc(node_p, 1)

            def multiply(ib, b, u, first):
                for j in range(UT):
                    t = u * UT + j
                    if first:
                        pe.wait_ge(split, t + 1)
                    pe.wait_ge(scaled, ib * TILES + (t + 1))
                    for h in range(DH):
                        for part in range(2):
                            i = pe.matmul(acc[b][h][:, :], g[:, t, part, h * P:(h + 1) * P], ms[:, t % SLOTS, :],
                                          start=(t == 0 and part == 0), stop=(t == TILES - 1 and part == 1))
                    i.then_inc(multiplied, 1)
                    if first:
                        for h in range(DH):
                            for part in range(2):
                                i = pe.matmul((pm, pm2)[h][:, 0:3], g[:, t, part, h * P:(h + 1) * P], cf[:, t, :],
                                              start=(t == 0 and part == 0), stop=(t == TILES - 1 and part == 1))
                        i.then_inc(node_sum, 1)

            def project(j, ks):
                pe.wait_ge(acc_copied, (j + 1) * DH)
                for k in ks:
                    if not (isinstance(j, int) and j == 0 and k < 2):
                        pe.wait_ge(hp_read, j * RT + (k - 1))
                    for h in range(DH):
                        i = pe.matmul(hp[k % 2][:, 0:D + 1], uT[:, h, k * P:(k + 1) * P], wa[:, h, :],
                                      start=(h == 0), stop=(h == DH - 1))
                    i.then_inc(projected, 1)

            def main(ib, b, prev):
                for u in range(UNITS):
                    if u == 0 and not (isinstance(ib, int) and ib < 2):
                        pe.wait_ge(acc_copied, (ib - 1) * DH)
                    multiply(ib, b, u, isinstance(ib, int) and ib == 0)
                    if prev and u == 1:
                        if isinstance(ib, int) and ib == 1:
                            pe.wait_ge(node_v, 6)
                            for h in range(DH):
                                i = pe.matmul(pm[:, D:2 * D], diag[:, h, :], wa[:, h, 0:D],
                                              start=(h == 0), stop=(h == DH - 1))
                            i.then_inc(node_p, 1)
                        project(ib - 1, (0, 1))
                    if prev and u == 4:
                        project(ib - 1, (2, 3))

            pe.wait_ge(g0_ready, 1)
            main(0, 0, False)
            main(1, 1, True)
            with pe.Fori(0, BLOCKS // 2 - 1) as k:
                for b in range(2):
                    main(2 * k + 2 + b, b, True)
            project(BLOCKS - 1, range(RT))

        @block.vector
        def _(dve):
            step = Chain(dve, v_step, 0)
            dve.memset(wg[:, :, :], 0.0).then_inc(consts_set, 1)
            step(dve.memset(wa[:, :, :], 0.0))
            dve.wait_ge(consts_set, 3)
            dve.tensor_copy(wa[:, 1, D:D + 1], ident[:, P - 1:P]).then_inc(consts_set, 1)

            def fold_weights():
                dve.wait_ge(weights_loaded, 16 * 5)
                for h in range(DH):
                    step(dve.scalar_tensor_tensor(out=junk_v[:, :], in0=wa[:, h, 0:D], scalar=1.0, in1=a2b[:, :],
                                                  op0=ALU.mult, op1=ALU.mult, accum_out=sc[:, 8 + h:9 + h]))
                dve.wait_ge(consts_set, 4)
                dve.tensor_scalar(diag[:, 0, :], ident[:, :], sc[:, 8:9], None, ALU.mult)
                dve.tensor_scalar(diag[:, 1, :], ident[:, :], sc[:, 9:10], None, ALU.mult).then_inc(prep_ready, 1)
                dve.wait_ge(prep_multiplied, DH)
                step(dve.tensor_copy(ub[:, :], pm[:, 0:D]))
                for h in range(DH):
                    step(dve.scalar_tensor_tensor(out=junk_v[:, 0:D - 1], in0=wg[:, h, 0:D - 1], scalar=1.0,
                                                  in1=ub[:, 0:D - 1], op0=ALU.mult, op1=ALU.mult,
                                                  accum_out=wg[:, h, D - 1:D]))
                dve.sem_inc(prep_ready, 1)

            s, d, cv, v, ve, sd = [c16[:, i, :] for i in range(6)]

            def statistics(c, ts, own):
                dve.wait_ge(x_loaded[c], 16 * QUAD)
                for t in ts:
                    i = dve.bn_stats(st[:, t, :], xz_t[:, bass.ds(c * CT + t, 1), :])
                own(i)

            def variance(c, own):
                dve.tensor_tensor(s, st[:, :, 1], st[:, :, 4], ALU.add)
                dve.tensor_tensor(d, st[:, :, 1], st[:, :, 4], ALU.subtract)
                own(dve.tensor_tensor(cv, st[:, :, 2], st[:, :, 5], ALU.add))
                own(dve.scalar_tensor_tensor(out=v, in0=d, scalar=0.25, in1=d, op0=ALU.mult, op1=ALU.mult))
                own(dve.scalar_tensor_tensor(out=v, in0=cv, scalar=1.0 / D, in1=v, op0=ALU.mult, op1=ALU.add))
                dve.tensor_scalar(ve, v, LN_EPS, None, ALU.add).then_inc(var_ready, 1)

            def scale_bias(c, own):
                cols = bass.ts(c, CT)
                dve.wait_ge(sd_ready, c + 1)
                own(dve.reciprocal(rstd[:, cols], sd))
                own(dve.scalar_tensor_tensor(out=nbias[:, cols], in0=s, scalar=-0.5, in1=rstd[:, cols],
                                             op0=ALU.mult, op1=ALU.mult))
                own(dve.tensor_tensor(q0[:, cols], xz_t[:, cols, 0], rstd[:, cols], ALU.mult))
                own(dve.tensor_tensor(q0[:, cols], q0[:, cols], nbias[:, cols], ALU.add))
                dve.tensor_scalar(q0[:, cols], q0[:, cols], THETA_MIN, None, ALU.max).then_inc(stats_ready, 1)

            def z_square(n, k):
                dve.wait_ge(z_multiplied, n + 1)
                dve.tensor_scalar(xz_t[:, bass.ds(2 * n, 2), :], zp[k % 2][:, :].rearrange("p (t d) -> p t d", d=D),
                                  1.0, None, ALU.mult).then_inc(z_copied, 1)
                dve.wait_ge(z_copied, n + 1)
                for e in range(2):
                    t = 2 * n + e
                    after(dve, z_squared, t)
                    dve.scalar_tensor_tensor(out=junk_v[:, 0:D - 1], in0=xz_t[:, bass.ds(t, 1), 0:D - 1],
                                             scalar=1.0, in1=xz_t[:, bass.ds(t, 1), 0:D - 1],
                                             op0=ALU.mult, op1=ALU.mult, accum_out=n2[:, bass.ds(t, 1)])\
                       .then_inc(z_squared, 1)

            def node_chunk(c, last=False):
                own = Chain(dve, v_chunk, (c + 1) * VCH)
                for k in range(CP):
                    n = c * CP + k
                    if not last and k < 3:
                        statistics(c + 1, range(3 * k, min(3 * k + 3, CT)), own)
                    if not last and k == 2:
                        variance(c + 1, own)
                    if not last and k == CP - 1:
                        scale_bias(c + 1, own)
                        assert own.n == VCH
                    z_square(n, k)

            own = Chain(dve, v_chunk, 0)
            for k in range(3):
                statistics(0, range(3 * k, min(3 * k + 3, CT)), own)
            variance(0, own)
            scale_bias(0, own)
            assert own.n == VCH
            fold_weights()
            for c in range(CHUNKS):
                node_chunk(c, last=(c == CHUNKS - 1))

            def turn_unit(ib, u):
                n = ib * UNITS + u
                q = u // 2
                if u % 2 == 0:
                    if not (isinstance(ib, int) and ib == 0 and q < NRAW):
                        dve.wait_ge(adj_loaded[q], (ib + 1) * (16 * QUAD))
                        dve.tensor_scalar(raw[q], raw[q], 0.0, None, ALU.is_gt).then_inc(is_set, 1)
                    dve.wait_ge(is_set, ib * QTR + (q + 1))
                if not (isinstance(ib, int) and ib == 0 and u < 2):
                    dve.wait_ge(scaled, (n - 1) * UT)
                src = raw[q].bitcast(U32).rearrange("p (g h m w) -> p h m g w", h=2, m=UM, w=B32)
                dve.transpose(mT[u % 2][:, :, :, :], src[:, u % 2]).then_inc(transposed, 1)

            dve.wait_ge(z_squared, TILES)
            dve.wait_ge(a_step, TILES)
            dve.wait_ge(stats_ready, CHUNKS)
            step(dve.tensor_scalar(tmp65, q0, 1.0, None, ALU.subtract))
            step(dve.scalar_tensor_tensor(out=tmp64, in0=q0, scalar=1.0, in1=tmp65, op0=ALU.add, op1=ALU.mult))
            step(dve.tensor_scalar(ny2, ny2, NORM_FLOOR2, None, ALU.max))
            dve.tensor_scalar(n2, n2, NORM_FLOOR2, None, ALU.max).then_inc(node_v, 1)
            dve.wait_ge(node_a, 3)
            dve.tensor_tensor(c_, q0, tmp64, ALU.add).then_inc(node_v, 1)
            step(dve.reciprocal(tmp65, ny2))
            step(dve.reciprocal(tmp64, n_))
            dve.wait_ge(node_a, 4)
            step(dve.scalar_tensor_tensor(out=c_, in0=c_, scalar=ACOSH_MIN, in1=tmp65, op0=ALU.max, op1=ALU.mult))
            step(dve.tensor_tensor(a_, c_, n_, ALU.mult))
            step(dve.tensor_scalar(a_, a_, ACOSH_MIN, None, ALU.max))
            step(dve.tensor_tensor(r_, a_, tmp64, ALU.mult))
            dve.tensor_tensor(tv, r_, xz_t[:, :, D - 1], ALU.mult).then_inc(r_ready, 1)
            dve.wait_ge(r_ready, 1)
            step(dve.tensor_reduce(sc[:, 0:1], tv, AX.X, ALU.max))
            step(dve.tensor_reduce(sc[:, 1:2], tv, AX.X, ALU.min))
            dve.tensor_scalar(sc[:, 1:2], sc[:, 1:2], -1.0, None, ALU.mult).then_inc(node_v, 1)
            turn_unit(0, 0)
            dve.wait_ge(node_p, 1)
            step(dve.tensor_reduce(sc[0:2, 2:3], pm2[0:2, 0:P], AX.X, ALU.max))
            dve.tensor_scalar(sc[0:2, 6:8], ident[0:2, 0:2], sc[0:2, 2:3], None, ALU.mult).then_inc(node_v, 1)
            dve.wait_ge(node_p, 2)
            dve.tensor_scalar(sc[:, 4:5], pm2[:, P:P + 1], -1.0, None, ALU.mult).then_inc(node_v, 1)
            turn_unit(0, 1)
            dve.wait_ge(node_a, 5)
            step(dve.scalar_tensor_tensor(out=tmp64, in0=a_, scalar=1.0, in1=w_, op0=ALU.max, op1=ALU.mult))
            step(dve.tensor_scalar(tmp64.bitcast(I32), tmp64.bitcast(I32), EXP_MASK, None, ALU.bitwise_and))
            step(dve.tensor_scalar(beta, tmp64, BETA, None, ALU.mult))
            step(dve.reciprocal(tmp65, beta))
            step(dve.tensor_tensor(gs, w_, tmp65, ALU.mult))
            dve.tensor_tensor(gr, gs, r_, ALU.mult).then_inc(w_ready, 1)
            step(dve.reciprocal(xz_t[:, :, D - 1], r_))
            step(dve.reciprocal(tmp65, gs))
            step(dve.tensor_copy(cf[:, :, 0], tmp65))
            step(dve.tensor_tensor(tmp65, tmp65, cf[:, :, 0], ALU.subtract))
            step(dve.tensor_copy(cf[:, :, 1], tmp65))
            dve.tensor_tensor(cf[:, :, 2], tmp65, cf[:, :, 1], ALU.subtract).then_inc(g0_ready, 1)
            dve.wait_ge(w_ready, 1)

            def split_tiles(u):
                for t in range(u * UT, (u + 1) * UT):
                    dve.tensor_scalar(g[:, t, 0, :], xz_t[:, t, :], gr[:, t:t + 1], None, ALU.mult)\
                       .then_inc(split_high, 1)
                for t in range(u * UT, (u + 1) * UT):
                    dve.wait_ge(split_high, t + 1)
                    dve.scalar_tensor_tensor(out=g[:, t, 1, :], in0=xz_t[:, t, :], scalar=gr[:, t:t + 1],
                                             in1=g[:, t, 0, :], op0=ALU.mult, op1=ALU.subtract).then_inc(split, 1)

            def root(own, dst, arg, half):
                dve.tensor_scalar(dst.bitcast(I32), arg.bitcast(I32), 0.5, SQRT_MAGIC, ALU.mult, ALU.add)
                own(dve.tensor_scalar(half, arg, 0.5, None, ALU.mult))
                rec = e8[:, 15, 0:dst.shape[1]]
                for _ in range(3):
                    own(dve.reciprocal(rec, dst))
                    own(dve.tensor_tensor(rec, rec, half, ALU.mult))
                    own(dve.scalar_tensor_tensor(out=dst, in0=dst, scalar=0.5, in1=rec, op0=ALU.mult, op1=ALU.add))

            def copy_acc(j, b):
                dve.wait_ge(multiplied, (j + 1) * TILES)
                after(dve, projected, j * RT)
                for h in range(DH):
                    dve.tensor_copy(uT[:, h, :], acc[b][h][:, :]).then_inc(acc_copied, 1)

            def normalise(j, b, ks):
                own = Chain(dve, v_norm, j * N_NORM + 4 * ks[0])
                for k in ks:
                    dve.wait_ge(projected, j * RT + (k + 1))
                    after(dve, tanh_ready, j * RT)
                    empty, den, rden = [e8[:, i, k:k + 1] for i in (1, 2, 3)]
                    own(dve.tensor_scalar(empty, hp[k % 2][:, D:D + 1], 0.0, None, ALU.is_equal))
                    own(dve.tensor_tensor(den, hp[k % 2][:, D:D + 1], empty, ALU.add))
                    own(dve.reciprocal(rden, den))
                    dve.scalar_tensor_tensor(out=hrow[:, k, :], in0=hmean[:, :], scalar=empty,
                                             in1=hp[k % 2][:, 0:D], op0=ALU.mult, op1=ALU.add).then_inc(hp_read, 1)
                    dve.wait_ge(hp_read, j * RT + (k + 1))
                    dve.tensor_scalar(erow[b][:, k, :], hrow[:, k, :], rden, 0.0, ALU.mult, ALU.min)\
                       .then_inc(neg_ready, 1)
                    own(dve.tensor_scalar(hrow[:, k, :], hrow[:, k, :], rden, 0.0, ALU.mult, ALU.max))
                assert own.n == 4 * len(ks)

            def elu(j, b):
                for k in range(RT):
                    dve.wait_ge(exp_ready, j * RT + (k + 1))
                    dve.scalar_tensor_tensor(out=hrow[:, k, :], in0=erow[b][:, k, :], scalar=-1.0, in1=hrow[:, k, :],
                                             op0=ALU.add, op1=ALU.add).then_inc(elu_ready, 1)

            def elu_norm(j):
                own = Chain(dve, v_root, j * N_ROOT)
                dve.wait_ge(elu_squared, (j + 1) * RT)
                own(dve.tensor_scalar(e8[:, 4, 0:RT], e8[:, 0, 0:RT], NORM_FLOOR2, None, ALU.max))
                own(dve.tensor_scalar(e8[:, 4, RT:2 * RT], e8[:, 0, 0:RT], 1.0, None, ALU.add))
                root(own, e8[:, 7, :], e8[:, 4, :], e8[:, 11, :])
                dve.tensor_tensor(e8[:, 5, 0:RT], e8[:, 7, 0:RT], e8[:, 7, RT:2 * RT], ALU.add).then_inc(ln_arg, 1)
                assert own.n == N_ROOT

            def tanh_scale(j):
                own = Chain(dve, v_scale, j * N_SCALE)
                own(dve.reciprocal(e8[:, 11, 0:RT], e8[:, 7, 0:RT]))
                own(dve.tensor_scalar(e8[:, 11, 0:RT], e8[:, 11, 0:RT], 0.5, None, ALU.mult))
                dve.wait_ge(ln_ready, j + 1)
                dve.scalar_tensor_tensor(out=e8[:, 6, 0:RT], in0=e8[:, 5, 0:RT], scalar=ACOSH_MIN,
                                         in1=e8[:, 11, 0:RT], op0=ALU.max, op1=ALU.mult).then_inc(scale_ready, 1)
                assert own.n == N_SCALE

            def sigmoid(j, b):
                own = Chain(dve, v_sig, j * N_SIG)
                for k in range(RT):
                    dve.wait_ge(tanh_ready, j * RT + (k + 1))
                    own(dve.tensor_scalar(erow[b][:, k, :], erow[b][:, k, :], 0.5, 0.5, ALU.mult, ALU.add))
                    own(dve.scalar_tensor_tensor(out=junk_v[:, 0:D - 1], in0=erow[b][:, k, 1:D], scalar=1.0,
                                                 in1=erow[b][:, k, 1:D], op0=ALU.mult, op1=ALU.mult,
                                                 accum_out=e8[:, 9, k:k + 1]))
                own(dve.tensor_scalar(e8[:, 9, 0:RT], e8[:, 9, 0:RT], NORM_FLOOR2, None, ALU.max))
                root(own, e8[:, 8, 0:RT], e8[:, 9, 0:RT], e8[:, 14, 0:RT])
                dve.reciprocal(e8[:, 14, 0:RT], e8[:, 8, 0:RT]).then_inc(norm_ready, 1)
                assert own.n == N_SIG

            def finish(j, pair, b):
                own = Chain(dve, v_fin, j * N_FIN)
                dve.wait_ge(norm_ready, j + 1)
                dve.wait_ge(cosh_ready, j + 1)
                dve.wait_ge(xt_loaded[b], (pair + 1) * 16)
                ex, inv, sh, ch, rn = [e8[:, i, 0:RT] for i in (10, 11, 12, 13, 14)]
                own(dve.reciprocal(inv, ex))
                own(dve.tensor_tensor(sh, ex, inv, ALU.subtract))
                own(dve.tensor_tensor(ch, ex, inv, ALU.add))
                own(dve.scalar_tensor_tensor(out=sh, in0=sh, scalar=0.5, in1=rn, op0=ALU.mult, op1=ALU.mult))
                for k in range(RT):
                    dve.scalar_tensor_tensor(out=xt[b][:, k, 1:D], in0=erow[b][:, k, 1:D], scalar=sh[:, k:k + 1],
                                             in1=xt[b][:, k, 1:D], op0=ALU.mult, op1=ALU.add)
                dve.scalar_tensor_tensor(out=xt[b][:, :, 0], in0=ch, scalar=0.5, in1=xt[b][:, :, 0],
                                         op0=ALU.mult, op1=ALU.add).then_inc(rows_ready, 1)
                assert own.n == N_FIN

            def mean_row():
                dve.wait_ge(node_sum, TILES)
                step(dve.tensor_reduce(sc[:, 10:11], pm[:, 0:3], AX.X, ALU.add))
                step(dve.tensor_reduce(sc[:, 11:12], pm2[:, 0:3], AX.X, ALU.add))
                dve.tensor_scalar(diag[:, 0, :], ones[:, :], sc[:, 10:11], 1.0 / N, ALU.mult, ALU.mult)
                dve.tensor_scalar(diag[:, 1, :], ones[:, :], sc[:, 11:12], 1.0 / N, ALU.mult, ALU.mult)\
                   .then_inc(node_v, 1)

            def main(ib, pair, b, prev, prev2):
                for u in range(UNITS):
                    turn_unit(ib, u)
                    if isinstance(ib, int) and ib == 1 and u == 3:
                        mean_row()
                    if isinstance(ib, int) and ib == 1 and u == 4:
                        dve.wait_ge(node_p, 3)
                        step(dve.tensor_copy(hmean[:, :], pm[:, D:2 * D]))
                    if prev2 and u == 1:
                        elu_norm(ib - 2)
                    if prev2 and u == 3:
                        tanh_scale(ib - 2)
                    if prev and u == 3:
                        copy_acc(ib - 1, 1 - b)
                    if prev and u == 4:
                        normalise(ib - 1, 1 - b, (0, 1))
                    if prev2 and u == 5:
                        sigmoid(ib - 2, b)
                    if prev and u == 6:
                        normalise(ib - 1, 1 - b, (2, 3))
                    if prev and u == 7:
                        elu(ib - 1, 1 - b)
                    if prev2 and u == 7:
                        finish(ib - 2, pair - 1, b)

            for u in range(UNITS):
                split_tiles(u)
                if u >= 2:
                    turn_unit(0, u)
            dve.wait_ge(split, TILES)
            main(1, 0, 1, True, False)
            with dve.Fori(0, BLOCKS // 2 - 1) as k:
                for b in range(2):
                    main(2 * k + 2 + b, k + 1, b, True, True)
            j = BLOCKS - 2
            elu_norm(j)
            tanh_scale(j)
            sigmoid(j, 0)
            finish(j, j // 2, 0)
            j = BLOCKS - 1
            copy_acc(j, 1)
            normalise(j, 1, (0, 1))
            normalise(j, 1, (2, 3))
            elu(j, 1)
            elu_norm(j)
            tanh_scale(j)
            sigmoid(j, 1)
            finish(j, j // 2, 1)


_INS = ["x", "adj", "L0_gnn_W_gcn", "L0_gnn_W_att", "L0_gnn_a_att"]


def kernel(**inputs):
    import numpy as _np
    import concourse.bacc as _bacc
    from concourse import mybir as _mybir
    from concourse.bass_utils import run_bass_kernel_spmd as _run

    nc = _bacc.Bacc("TRN2", target_bir_lowering=False, num_devices=1)
    arrays, args = {}, []
    for name in _INS:
        a = _np.ascontiguousarray(inputs[name])
        arrays[f"in_{name}"] = a
        args.append(nc.dram_tensor(f"in_{name}", a.shape, _mybir.dt.from_np(a.dtype), kind="ExternalInput").ap())
    args.append(nc.dram_tensor("out_rows", inputs["x"].shape, _mybir.dt.float32, kind="ExternalOutput").ap())
    gnn_kernel(nc, *args)
    r = _run(nc, [arrays], core_ids=[0])
    return r.results[0]["out_rows"]
```

```python
import math
from contextlib import ExitStack

import concourse.bass as bass
from concourse import mybir


ALU = mybir.AluOpType
ACT = mybir.ActivationFunctionType
AX = mybir.AxisListType
F32 = mybir.dt.float32
BF16 = mybir.dt.bfloat16
F16 = mybir.dt.float16
U32 = mybir.dt.uint32
I32 = mybir.dt.int32

P = 128
QUAD = 4
B32 = P // QUAD
LN_EPS = 1e-5
NORM_FLOOR2 = 1e-30
THETA_MIN = 1.0 + 2.0 ** -23
ACOSH_MIN = math.acosh(THETA_MIN)
EXP_MASK = 0x7F800000
BETA = 2.0 ** -14
WIDE_T = 64.0
WIDE_NORM = 1024.0
MASK_FILL = -2.0 ** 53
INVERSE_BITS = float((254 + 14) << 23)
SQRT_MAGIC = float(0x1FBD1DF5)


def after(eng, sem, value):
    if not (isinstance(value, int) and value <= 0):
        eng.wait_ge(sem, value)


class Chain:

    def __init__(self, eng, sem, base):
        self.eng, self.sem, self.base, self.n = eng, sem, base, 0

    def __call__(self, ins):
        ins.then_inc(self.sem, 1)
        self.n += 1
        self.settle()

    def go(self, ins):
        ins.then_inc(self.sem, 1)
        self.n += 1

    def settle(self, but=0):
        self.eng.wait_ge(self.sem, self.base + self.n - but)


def gnn_kernel(nc, x, adj, w_gcn, w_att, a_att, out):
    N, D = x.shape
    DH = D // P
    NQ = N // QUAD
    TILES = N // P
    CHUNKS = 8
    CT = TILES // CHUNKS
    CP = CT // 2
    IB = 512
    BLOCKS = N // IB
    G32 = IB // B32
    QTR = 4
    QN = NQ // QTR
    UNITS = 2 * QTR
    UT = TILES // UNITS
    UM = UT // 2
    SLOTS = 2 * UT
    RT = IB // P

    with ExitStack() as ctx:
        def sb(name, shape, dt):
            return ctx.enter_context(nc.sbuf_tensor(name, shape, dt))

        def pb(name, shape, dt=F32):
            return ctx.enter_context(nc.psum_tensor(name, shape, dt))

        def sem(name):
            return ctx.enter_context(nc.semaphore(name))

        xz = sb("xz", [P, TILES * D], F32)
        xz_t = xz[:, :].rearrange("p (t d) -> p t d", d=D)
        LOADF = G32 * QN // 2
        NRAW = 2
        raw = [sb(f"raw{i}", [P, G32 * QN], BF16)[:, :] for i in range(NRAW)]
        raw += [xz[:, i * LOADF:(i + 1) * LOADF].bitcast(BF16) for i in range(QTR - NRAW)]
        rest = (QTR - NRAW) * LOADF

        def row_buffer(i):
            return xz[:, rest + i * RT * D:rest + (i + 1) * RT * D]

        uT = row_buffer(0).rearrange("p (h i) -> p h i", h=DH)
        hrow, *erow = [row_buffer(i).rearrange("p (k d) -> p k d", d=D) for i in (1, 2, 3)]
        xt = [row_buffer(i).rearrange("p (k d) -> p k d", d=D) for i in (4, 5)]
        gbuf = sb("gbuf", [P, TILES * 2 * D], F16)
        g = gbuf[:, :].rearrange("p (t s d) -> p t s d", s=2, d=D)
        ring = gbuf[:, 0:4 * 4 * D * 2].bitcast(F32)
        hb = [ring[:, i * 2 * D:(i + 1) * 2 * D].rearrange("p (e d) -> p e d", e=2) for i in range(2)]
        hT = [ring[:, (2 + i) * 2 * D:(3 + i) * 2 * D].rearrange("p (h e j) -> p h e j", h=DH, e=2) for i in range(2)]
        prep = gbuf[:, 4 * 4 * D * 2:4 * 4 * D * 2 + 4 * D].bitcast(F32)
        a2b, ub = prep[:, 0:D], prep[:, D:2 * D]
        mT = [sb(f"mT{i}", [P, UM, G32, B32], U32) for i in range(2)]
        ms = sb("ms", [P, SLOTS, IB], BF16)
        wg = sb("wg", [P, DH, D], F32)
        wa = sb("wa", [P, DH, D + 1], F32)
        wide_flag = sb("wide_flag", [P, 1], I32)
        cf = sb("cf", [P, TILES, 3], BF16)
        ident = sb("ident", [P, P], F32)
        ones = sb("ones", [P, P], F32)
        diag = sb("diag", [P, DH, P], F32)
        hmean = sb("hmean", [P, D], F32)
        junk_v = sb("junk_v", [P, 2, D], F32)
        junk_a = sb("junk_a", [P, D], F32)
        st = sb("st", [P, CT, 6], F32)
        c16 = sb("c16", [P, 8, CT], F32)
        s64 = sb("s64", [P, 16, TILES], F32)
        (rstd, nbias, q0, ny2, n2, c_, n_, a_, r_, w_, beta, gs, gr, tv, tmp64, tmp65) = [s64[:, i, :] for i in range(16)]
        sc = sb("sc", [P, 16], F32)
        e8 = sb("e8", [P, 16, 8], F32)

        h32 = gbuf[:, :].bitcast(F32).rearrange("p (t d) -> p t d", d=D)
        wide = ms[:, :, :].bitcast(F32)
        fill, logit, best, top_row = [wide[:, 2 * i:2 * i + 2, :].rearrange("p a b -> p (a b)") for i in range(4)]
        weight = [wide[:, 2 * i:2 * i + 2, :].rearrange("p a b -> p (a b)") for i in (4, 5)]
        diag_top = wide[:, 12:14, :].rearrange("p a b -> p (a b)")

        acc = [[pb(f"acc{b}{h}", [P, IB]) for h in range(DH)] for b in range(2)]
        hp = [pb(f"hp{i}", [P, 512]) for i in range(RT)]
        pm, pm2 = hp[3], hp[2]
        hTp = [acc[0][i] for i in range(2)]
        zp = [acc[1][i] for i in range(2)]

        consts_set = sem("consts_set")
        ident_cleared = sem("ident_cleared")
        weights_loaded = sem("weights_loaded")
        x_loaded = [sem(f"x_loaded{c}") for c in range(CHUNKS)]
        prep_ready = sem("prep_ready")
        prep_multiplied = sem("prep_multiplied")
        var_ready = sem("var_ready")
        sd_ready = sem("sd_ready")
        stats_ready = sem("stats_ready")
        q_ready = sem("q_ready")
        h_ready = sem("h_ready")
        h_transposed = sem("h_transposed")
        hT_copied = sem("hT_copied")
        z_multiplied = sem("z_multiplied")
        z_copied = sem("z_copied")
        z_squared = sem("z_squared")
        v_step = sem("v_step")
        r_ready = sem("r_ready")
        v_chunk = sem("v_chunk")
        v_norm = sem("v_norm")
        v_root = sem("v_root")
        v_scale = sem("v_scale")
        v_sig = sem("v_sig")
        v_fin = sem("v_fin")
        a_step = sem("a_step")
        node_v = sem("node_v")
        node_a = sem("node_a")
        node_p = sem("node_p")
        beta_ready = sem("beta_ready")
        w_ready = sem("w_ready")
        node_sum = sem("node_sum")
        split_high = sem("split_high")
        split_high_a = sem("split_high_a")
        split = sem("split")
        cf_ready = sem("cf_ready")
        flag_ready = sem("flag_ready")
        wide_free = sem("wide_free")
        v_wide = sem("v_wide")
        v_wide_set = sem("v_wide_set")
        best_ready = sem("best_ready")
        best_turned = sem("best_turned")
        top_ready = sem("top_ready")
        top_spread = sem("top_spread")
        logit_ready = sem("logit_ready")
        weight_ready = sem("weight_ready")
        adj_loaded = [sem(f"adj_loaded{i}") for i in range(QTR)]
        is_set = sem("is_set")
        transposed = sem("transposed")
        scaled = sem("scaled")
        multiplied = sem("multiplied")
        acc_copied = sem("acc_copied")
        projected = sem("projected")
        hp_read = sem("hp_read")
        neg_ready = sem("neg_ready")
        exp_ready = sem("exp_ready")
        elu_ready = sem("elu_ready")
        elu_squared = sem("elu_squared")
        ln_arg = sem("ln_arg")
        ln_ready = sem("ln_ready")
        scale_ready = sem("scale_ready")
        tanh_ready = sem("tanh_ready")
        norm_ready = sem("norm_ready")
        cosh_ready = sem("cosh_ready")
        rows_ready = sem("rows_ready")
        xt_loaded = [sem(f"xt_loaded{i}") for i in range(2)]
        stored = [sem(f"stored{i}") for i in range(2)]

        x_nodes = x.rearrange("(a m w e) d -> a w m (e d)", a=QUAD, w=B32, e=2)
        x_rows = x.rearrange("(b k p) d -> b p k d", k=RT, p=P)
        out_rows = out.rearrange("(b k p) d -> b p k d", k=RT, p=P)
        adj_v = adj.rearrange("(b g i) (a n) -> b a i g n", g=G32, i=B32, a=QUAD)
        N_NORM, N_ROOT, N_SCALE, N_SIG, N_FIN = 12, 12, 2, 2 * RT + 11, 4

        def high_by_act(t):
            return t >= 2 * UT and t % UM >= UM // 2

        def highs(t, by_act):
            return sum(high_by_act(i) == by_act for i in range(t + 1))

        block = ctx.enter_context(nc.Block())

        @block.sync
        def _(sp):
            def load_x(c):
                for a in range(QUAD):
                    dst = xz_t[a * B32:(a + 1) * B32, bass.ts(c, CT), :]
                    sp.dma_start(dst.rearrange("p (m e) d -> p m (e d)", e=2),
                                 x_nodes[a, :, bass.ts(c, CP), :]).then_inc(x_loaded[c], 16)

            load_x(0)
            sp.wait_ge(consts_set, 4)
            sp.dma_start(wg[1:P, 0, 0:D - 1], w_gcn[0:P - 1, :]).then_inc(weights_loaded, 16)
            sp.dma_start(wg[:, 1, 0:D - 1], w_gcn[P - 1:D - 1, :]).then_inc(weights_loaded, 16)
            sp.dma_start(wa[:, 0, 0:D], w_att[1:P + 1, :]).then_inc(weights_loaded, 16)
            sp.dma_start(wa[0:P - 1, 1, 0:D], w_att[P + 1:D, :]).then_inc(weights_loaded, 16)
            sp.dma_start(a2b[:, :], a_att[D:2 * D, :].rearrange("d o -> o d").to_broadcast([P, D]))\
              .then_inc(weights_loaded, 16)
            for c in range(1, CHUNKS):
                load_x(c)

            def load_rows(j, b):
                sp.dma_start(xt[b][:, :, :], x_rows[j, :, :, :]).then_inc(xt_loaded[b], 16)

            def store_rows(j, b):
                sp.wait_ge(rows_ready, j + 1)
                sp.dma_start(out_rows[j, :, :, :], xt[b][:, :, :]).then_inc(stored[b], 16)

            sp.wait_ge(flag_ready, 1)
            is_wide = sp.value_load(wide_flag[0:1, 0:1])
            with sp.If(is_wide == 0):
                sp.wait_ge(split, TILES)
                load_rows(0, 0)
                load_rows(1, 1)
                with sp.Fori(0, BLOCKS // 2 - 1) as k:
                    for b in range(2):
                        store_rows(2 * k + b, b)
                        sp.wait_ge(stored[b], 16 * (k + 1))
                        load_rows(2 * k + 2 + b, b)
                for b in range(2):
                    store_rows(BLOCKS - 2 + b, b)
                for b in range(2):
                    sp.wait_ge(stored[b], 16 * (BLOCKS // 2))
            with sp.Else():
                sp.wait_ge(wide_free, 1)
                load_rows(0, 0)
                with sp.Fori(0, BLOCKS - 1) as j:
                    store_rows(j, 0)
                    sp.wait_ge(stored[0], 16 * (j + 1))
                    load_rows(j + 1, 0)
                store_rows(BLOCKS - 1, 0)
                sp.wait_ge(stored[0], 16 * BLOCKS)

        @block.gpsimd
        def _(pool):
            pool.memset(ident[:, :], 0.0).then_inc(ident_cleared, 1)
            pool.wait_ge(ident_cleared, 1)
            pool.affine_select(out=ident[:, :], in_=ident[:, :], compare_op=ALU.not_equal, fill=1.0, base=0,
                               pattern=[[-1, P]], channel_multiplier=1).then_inc(consts_set, 1)
            pool.memset(ones[:, :], 1.0).then_inc(consts_set, 1)

            def load_adj(ib, q):
                for a in range(QUAD):
                    dst = raw[q][a * B32:(a + 1) * B32, :].rearrange("p (g n) -> p g n", g=G32)
                    pool.dma_start(dst, adj_v[ib, a, :, :, q * QN:(q + 1) * QN]).then_inc(adj_loaded[q], 16)

            pool.wait_ge(x_loaded[CHUNKS // 2], 16 * QUAD)
            for q in range(NRAW):
                load_adj(0, q)
            for q in range(NRAW):
                pool.wait_ge(adj_loaded[q], 16 * QUAD)
                pool.tensor_scalar(raw[q], raw[q], 0.0, None, ALU.is_gt).then_inc(is_set, 1)
            pool.wait_ge(flag_ready, 1)
            is_wide = pool.value_load(wide_flag[0:1, 0:1])
            with pool.If(is_wide == 0):
                for q in range(NRAW, QTR):
                    pool.wait_ge(split, (q - NRAW + 1) * (TILES // QTR))
                    load_adj(0, q)
                with pool.Fori(1, BLOCKS) as ib:
                    for q in range(QTR):
                        pool.wait_ge(transposed, ib * UNITS + (2 * (q + 1) - UNITS))
                        load_adj(ib, q)
            with pool.Else():
                with pool.Fori(0, BLOCKS) as ib:
                    for q in range(QTR):
                        pool.wait_ge(wide_free, ib + 1)
                        load_adj(ib, q)

        @block.scalar
        def _(act):
            def deviation(c):
                act.wait_ge(var_ready, c + 1)
                act.activation(c16[:, 5, :], c16[:, 4, :], ACT.Sqrt).then_inc(sd_ready, 1)

            def h_tiles(n, k):
                after(act, h_transposed, n - 1)
                after(act, a_step, 2 * (n - 1))
                for e in range(2):
                    t = 2 * n + e
                    act.activation(hb[k % 2][:, e, :], xz_t[:, t, :], ACT.Relu,
                                   bias=nbias[:, t:t + 1], scale=rstd[:, t:t + 1]).then_inc(h_ready, 1)

            def h_square(n, k):
                act.wait_ge(h_ready, 2 * n + 2)
                for t in (2 * n, 2 * n + 1):
                    after(act, a_step, t)
                    act.activation(junk_a[:, 0:D - 1], hb[k % 2][:, t % 2, 1:D], ACT.Square,
                                   accum_out=ny2[:, t:t + 1]).then_inc(a_step, 1)

            def hT_copy(n, k):
                act.wait_ge(h_transposed, n + 1)
                after(act, z_multiplied, n - 1)
                act.activation(hT[k % 2], hTp[k % 2][:, :].rearrange("p (h e j) -> p h e j", h=DH, e=2),
                               ACT.Copy).then_inc(hT_copied, 1)

            def node_chunk(c, last=False):
                for k in range(CP):
                    n = c * CP + k
                    if k == CP - 1 and not last:
                        act.wait_ge(stats_ready, c + 2)
                    if not (last and k == CP - 1):
                        h_tiles(n + 1, k + 1)
                    h_square(n, k)
                    if k == 1 and not last:
                        deviation(c + 1)
                    hT_copy(n, k)
                    if k == 0 and last:
                        act.wait_ge(node_v, 1)
                        act.activation(tmp64, tmp64, ACT.Sqrt).then_inc(node_a, 1)

            deviation(0)
            act.wait_ge(stats_ready, 1)
            h_tiles(0, 0)
            for c in range(CHUNKS):
                node_chunk(c, last=(c == CHUNKS - 1))

            act.wait_ge(node_v, 2)
            act.activation(c_, c_, ACT.Ln).then_inc(node_a, 1)
            act.wait_ge(node_v, 3)
            act.activation(ny2, ny2, ACT.Sqrt).then_inc(node_a, 1)
            act.wait_ge(node_v, 4)
            act.activation(n_, n2, ACT.Sqrt).then_inc(node_a, 1)
            act.wait_ge(node_v, 7)
            act.activation(w_, tv, ACT.Exp, bias=sc[:, 4:5]).then_inc(node_a, 1)

            def scale_unit(ib, u):
                n = ib * UNITS + u
                act.wait_ge(transposed, n + 1)
                if not (isinstance(ib, int) and ib == 0 and u < 2):
                    act.wait_ge(multiplied, (n - 1) * UT)
                mv = mT[u % 2][:, :, :, :].bitcast(BF16)
                for j in range(UT):
                    src = mv[:, j // 2, :, :].rearrange("p g (i e) -> p (g i) e", e=2)[:, :, j % 2]
                    act.activation(ms[:, (u % 2) * UT + j, :], src, ACT.Copy,
                                   scale=beta[:, u * UT + j:u * UT + j + 1]).then_inc(scaled, 1)

            def high_parts(ts):
                act.wait_ge(w_ready, 1)
                for t in ts:
                    if high_by_act(t):
                        act.activation(g[:, t, 0, :], xz_t[:, t, :], ACT.Copy, scale=gr[:, t:t + 1])\
                           .then_inc(split_high_a, 1)

            def exp_rows(j, b):
                for k in range(RT):
                    act.wait_ge(neg_ready, j * RT + (k + 1))
                    act.activation(erow[b][:, k, :], erow[b][:, k, :], ACT.Exp).then_inc(exp_ready, 1)

            def square_rows(j, b, serial=False):
                for k in range(RT):
                    act.wait_ge(elu_ready, j * RT + (k + 1))
                    if not (serial and k == 0):
                        after(act, elu_squared, j * RT + k)
                    act.activation(junk_a[:, 0:D - 1], hrow[:, k, 1:D], ACT.Square,
                                   accum_out=e8[:, 0, k:k + 1]).then_inc(elu_squared, 1)

            def ln_rows(j, b):
                act.wait_ge(ln_arg, j + 1)
                act.activation(e8[:, 5, 0:RT], e8[:, 5, 0:RT], ACT.Ln).then_inc(ln_ready, 1)

            def tanh_rows(j, b):
                act.wait_ge(scale_ready, j + 1)
                for k in range(RT):
                    act.activation(erow[b][:, k, :], hrow[:, k, :], ACT.Tanh,
                                   scale=e8[:, 6, k:k + 1]).then_inc(tanh_ready, 1)

            def cosh_rows(j, b):
                act.wait_ge(norm_ready, j + 1)
                act.activation(e8[:, 10, 0:RT], e8[:, 8, 0:RT], ACT.Exp).then_inc(cosh_ready, 1)

            early = {5: exp_rows, 7: square_rows}
            late = {2: ln_rows, 3: tanh_rows, 5: cosh_rows}
            early_last = {4: exp_rows, 5: square_rows, 6: ln_rows, 7: tanh_rows}

            def main(ib, b, prev, prev2, last=False):
                for u in range(UNITS):
                    if isinstance(ib, int) and ib == 0 and 1 <= u < UNITS - 1:
                        high_parts(range((u + 1) * UT, (u + 2) * UT))
                    scale_unit(ib, u)
                    if prev2 and u in late:
                        late[u](ib - 2, b)
                    if prev and u in (early_last if last else early):
                        (early_last if last else early)[u](ib - 1, 1 - b)

            act.wait_ge(flag_ready, 1)
            is_wide = act.value_load(wide_flag[0:1, 0:1])
            with act.If(is_wide == 0):
                act.wait_ge(beta_ready, 1)
                main(0, 0, False, False)
                main(1, 1, True, False)
                with act.Fori(0, BLOCKS // 2 - 2) as k:
                    for b in range(2):
                        main(2 * k + 2 + b, b, True, True)
                main(BLOCKS - 2, 0, True, True)
                main(BLOCKS - 1, 1, True, True, last=True)
                cosh_rows(BLOCKS - 2, 0)
                act.wait_ge(multiplied, BLOCKS * TILES)
                act.wait_ge(projected, (BLOCKS - 1) * RT)
                act.activation(uT[:, DH - 1, :], acc[1][DH - 1][:, :], ACT.Copy).then_inc(acc_copied, 1)
                for f in (*early.values(), *late.values()):
                    f(BLOCKS - 1, 1)
            with act.Else():
                with act.Fori(0, BLOCKS) as j:
                    for t in range(TILES):
                        act.wait_ge(logit_ready, j * TILES + (t + 1))
                        act.activation(weight[t % 2], weight[t % 2], ACT.Exp).then_inc(weight_ready, 1)
                    exp_rows(j, 0)
                    square_rows(j, 0, serial=True)
                    ln_rows(j, 0)
                    tanh_rows(j, 0)
                    cosh_rows(j, 0)

        @block.tensor
        def _(pe):
            pe.wait_ge(consts_set, 4)
            pe.wait_ge(prep_ready, 1)
            for h in range(DH):
                pe.matmul(pm[:, h * P:(h + 1) * P], ones[:, :], diag[:, h, :], start=True, stop=True)\
                  .then_inc(prep_multiplied, 1)

            def turn(n, k):
                pe.wait_ge(h_ready, 2 * n + 2)
                after(pe, hT_copied, n - 1)
                for h in range(DH):
                    for e in range(2):
                        i = pe.transpose(hTp[k % 2][:, (h * 2 + e) * P:(h * 2 + e + 1) * P],
                                         hb[k % 2][:, e, h * P:(h + 1) * P], ident[:, :])
                i.then_inc(h_transposed, 1)

            def mult(n, k):
                pe.wait_ge(hT_copied, n + 1)
                after(pe, z_copied, n - 1)
                for e in range(2):
                    for h in range(DH):
                        i = pe.matmul(zp[k % 2][:, e * D:(e + 1) * D], hT[k % 2][:, h, e, :], wg[:, h, :],
                                      start=(h == 0), stop=(h == DH - 1))
                i.then_inc(z_multiplied, 1)

            def node_chunk(c, last=False):
                for k in range(CP):
                    if not (last and k == CP - 1):
                        turn(c * CP + k + 1, k + 1)
                    mult(c * CP + k, k)

            turn(0, 0)
            pe.wait_ge(prep_ready, 2)
            for c in range(CHUNKS):
                node_chunk(c, last=(c == CHUNKS - 1))

            pe.wait_ge(node_v, 5)
            pe.transpose(pm2[0:3, 0:P], sc[:, 0:3], ident[:, :]).then_inc(node_p, 1)
            pe.wait_ge(node_v, 6)
            pe.matmul(pm2[:, P:P + 3], ones[0:3, :], sc[0:3, 5:8], start=True, stop=True).then_inc(node_p, 1)

            def multiply(ib, b, u, first):
                for j in range(UT):
                    t = u * UT + j
                    if first:
                        pe.wait_ge(split, t + 1)
                    pe.wait_ge(scaled, ib * TILES + (t + 1))
                    for h in range(DH):
                        for part in range(2):
                            i = pe.matmul(acc[b][h][:, :], g[:, t, part, h * P:(h + 1) * P], ms[:, t % SLOTS, :],
                                          start=(t == 0 and part == 0), stop=(t == TILES - 1 and part == 1))
                    i.then_inc(multiplied, 1)
                if first:
                    if u == 0:
                        pe.wait_ge(cf_ready, 1)
                    for t in range(u * UT, (u + 1) * UT):
                        for h in range(DH):
                            for part in range(2):
                                i = pe.matmul((pm, pm2)[h][:, 0:3], g[:, t, part, h * P:(h + 1) * P], cf[:, t, :],
                                              start=(t == 0 and part == 0), stop=(t == TILES - 1 and part == 1))
                    i.then_inc(node_sum, 1)

            def project(j, ks, serial=False):
                pe.wait_ge(acc_copied, (j + 1) * DH)
                for k in ks:
                    if isinstance(j, int) and j == 0:
                        if k == 3:
                            pe.wait_ge(node_v, 9)
                    elif not serial:
                        pe.wait_ge(hp_read, (j - 1) * RT + (k + 1))
                    for h in range(DH):
                        i = pe.matmul(hp[k][:, 0:D + 1], uT[:, h, k * P:(k + 1) * P], wa[:, h, :],
                                      start=(h == 0), stop=(h == DH - 1))
                    i.then_inc(projected, 1)

            def main(ib, b, prev, last=False):
                for u in range(UNITS):
                    if u == 0 and not (isinstance(ib, int) and ib < 2):
                        pe.wait_ge(acc_copied, (ib - 1) * DH)
                    multiply(ib, b, u, isinstance(ib, int) and ib == 0)
                    if prev and u == 1:
                        if isinstance(ib, int) and ib == 1:
                            pe.wait_ge(node_v, 8)
                            for h in range(DH):
                                i = pe.matmul(pm[:, D:2 * D], diag[:, h, :], wa[:, h, 0:D],
                                              start=(h == 0), stop=(h == DH - 1))
                            i.then_inc(node_p, 1)
                        project(ib - 1, range(RT) if last else (0, 1))
                    if prev and u == 4 and not last:
                        project(ib - 1, (2, 3))

            pe.wait_ge(flag_ready, 1)
            is_wide = pe.value_load(wide_flag[0:1, 0:1])
            with pe.If(is_wide == 0):
                main(0, 0, False)
                main(1, 1, True)
                with pe.Fori(0, BLOCKS // 2 - 2) as k:
                    for b in range(2):
                        main(2 * k + 2 + b, b, True)
                main(BLOCKS - 2, 0, True)
                main(BLOCKS - 1, 1, True, last=True)
                project(BLOCKS - 1, range(RT))
            with pe.Else():
                with pe.Fori(0, BLOCKS) as j:
                    pe.wait_ge(best_ready, j + 1)
                    for k in range(RT):
                        i = pe.transpose(hp[0][:, k * P:(k + 1) * P], best[:, k * P:(k + 1) * P], ident[:, :])
                    i.then_inc(best_turned, 1)
                    pe.wait_ge(top_ready, j + 1)
                    pe.matmul(hp[1][:, :], ones[:, :], diag_top, start=True, stop=True).then_inc(top_spread, 1)
                    for t in range(TILES):
                        pe.wait_ge(weight_ready, j * TILES + (t + 1))
                        for h in range(DH):
                            i = pe.matmul(acc[0][h][:, :], h32[:, t, h * P:(h + 1) * P], weight[t % 2],
                                          start=(t == 0), stop=(t == TILES - 1))
                        i.then_inc(multiplied, 1)
                    project(j, range(RT), serial=True)

        @block.vector
        def _(dve):
            step = Chain(dve, v_step, 0)
            dve.memset(wg[:, :, :], 0.0).then_inc(consts_set, 1)
            step(dve.memset(wa[:, :, :], 0.0))
            dve.wait_ge(consts_set, 3)
            dve.tensor_copy(wa[:, 1, D:D + 1], ident[:, P - 1:P]).then_inc(consts_set, 1)

            def fold_weights():
                dve.wait_ge(weights_loaded, 16 * 5)
                for h in range(DH):
                    step(dve.scalar_tensor_tensor(out=junk_v[:, h, :], in0=wa[:, h, 0:D], scalar=1.0, in1=a2b[:, :],
                                                  op0=ALU.mult, op1=ALU.mult, accum_out=sc[:, 8 + h:9 + h]))
                dve.wait_ge(consts_set, 4)
                dve.tensor_scalar(diag[:, 0, :], ident[:, :], sc[:, 8:9], None, ALU.mult)
                dve.tensor_scalar(diag[:, 1, :], ident[:, :], sc[:, 9:10], None, ALU.mult).then_inc(prep_ready, 1)
                dve.wait_ge(prep_multiplied, DH)
                step(dve.tensor_copy(ub[:, :], pm[:, 0:D]))
                for h in range(DH):
                    step(dve.scalar_tensor_tensor(out=junk_v[:, h, 0:D - 1], in0=wg[:, h, 0:D - 1], scalar=1.0,
                                                  in1=ub[:, 0:D - 1], op0=ALU.mult, op1=ALU.mult,
                                                  accum_out=wg[:, h, D - 1:D]))
                dve.sem_inc(prep_ready, 1)

            s, d, cv, v, ve, sd = [c16[:, i, :] for i in range(6)]

            own = Chain(dve, v_chunk, 0)

            def statistics(c, ts):
                for t in ts:
                    i = dve.bn_stats(st[:, t, :], xz_t[:, c * CT + t, :])
                own.go(i)

            def mean_parts():
                own.settle()
                dve.tensor_tensor(s, st[:, :, 1], st[:, :, 4], ALU.add)
                dve.tensor_tensor(d, st[:, :, 1], st[:, :, 4], ALU.subtract)
                own.go(dve.tensor_tensor(cv, st[:, :, 2], st[:, :, 5], ALU.add))

            def mean_square():
                own.settle()
                own.go(dve.scalar_tensor_tensor(out=v, in0=d, scalar=0.25, in1=d, op0=ALU.mult, op1=ALU.mult))

            def variance():
                own.settle()
                own.go(dve.scalar_tensor_tensor(out=v, in0=cv, scalar=1.0 / D, in1=v, op0=ALU.mult, op1=ALU.add))

            def variance_eps():
                own.settle()
                dve.tensor_scalar(ve, v, LN_EPS, None, ALU.add).then_inc(var_ready, 1)

            def scale(c):
                dve.wait_ge(sd_ready, c + 1)
                own.go(dve.reciprocal(rstd[:, c * CT:(c + 1) * CT], sd))

            def bias(c):
                own.settle()
                cols = slice(c * CT, (c + 1) * CT)
                dve.scalar_tensor_tensor(out=nbias[:, cols], in0=s, scalar=-0.5, in1=rstd[:, cols],
                                         op0=ALU.mult, op1=ALU.mult).then_inc(stats_ready, 1)
                own.go(dve.tensor_tensor(q0[:, cols], xz_t[:, cols, 0], rstd[:, cols], ALU.mult))

            def time_shift(c):
                cols = slice(c * CT, (c + 1) * CT)
                own.settle()
                dve.wait_ge(stats_ready, c + 1)
                own.go(dve.tensor_tensor(q0[:, cols], q0[:, cols], nbias[:, cols], ALU.add))

            def time_clip(c):
                cols = slice(c * CT, (c + 1) * CT)
                own.settle()
                dve.tensor_scalar(q0[:, cols], q0[:, cols], THETA_MIN, None, ALU.max).then_inc(q_ready, 1)

            def z_copy(n, k):
                dve.wait_ge(z_multiplied, n + 1)
                dve.tensor_scalar(xz_t[:, 2 * n:2 * n + 2, :], zp[k % 2][:, :].rearrange("p (t d) -> p t d", d=D),
                                  1.0, None, ALU.mult).then_inc(z_copied, 1)

            def z_square(t):
                dve.wait_ge(z_copied, t // 2 + 1)
                after(dve, z_squared, t - 1)
                dve.scalar_tensor_tensor(out=junk_v[:, t % 2, 0:D - 1], in0=xz_t[:, t, 0:D - 1], scalar=1.0,
                                         in1=xz_t[:, t, 0:D - 1], op0=ALU.mult, op1=ALU.mult,
                                         accum_out=n2[:, t:t + 1]).then_inc(z_squared, 1)

            def q_square(part):
                if part == 0:
                    step.go(dve.tensor_scalar(tmp65, q0, 1.0, None, ALU.subtract))
                else:
                    step.settle()
                    dve.scalar_tensor_tensor(out=tmp64, in0=q0, scalar=1.0, in1=tmp65, op0=ALU.add, op1=ALU.mult)\
                       .then_inc(node_v, 1)

            def q_sum():
                dve.wait_ge(node_a, 1)
                dve.tensor_tensor(c_, q0, tmp64, ALU.add).then_inc(node_v, 1)

            def y_floor():
                dve.wait_ge(a_step, TILES)
                dve.tensor_scalar(ny2, ny2, NORM_FLOOR2, None, ALU.max).then_inc(node_v, 1)

            def turn_unit(ib, u):
                n = ib * UNITS + u
                q = u // 2
                if u % 2 == 0:
                    if not (isinstance(ib, int) and ib == 0 and q < NRAW):
                        dve.wait_ge(adj_loaded[q], (ib + 1) * (16 * QUAD))
                        dve.tensor_scalar(raw[q], raw[q], 0.0, None, ALU.is_gt).then_inc(is_set, 1)
                    dve.wait_ge(is_set, ib * QTR + (q + 1))
                if not (isinstance(ib, int) and ib == 0 and u < 2):
                    dve.wait_ge(scaled, (n - 1) * UT)
                src = raw[q].bitcast(U32).rearrange("p (g h m w) -> p h m g w", h=2, m=UM, w=B32)
                dve.transpose(mT[u % 2][:, :, :, :], src[:, u % 2]).then_inc(transposed, 1)

            dve.wait_ge(x_loaded[0], 16 * QUAD)
            statistics(0, range(CT))
            mean_parts()
            mean_square()
            variance()
            variance_eps()
            scale(0)
            bias(0)
            time_shift(0)
            time_clip(0)
            fold_weights()
            dve.wait_ge(x_loaded[1], 16 * QUAD)
            statistics(1, range(CT))
            mean_parts()
            mean_square()
            variance()
            variance_eps()
            for c in range(CHUNKS):
                for k in range(CP):
                    n = c * CP + k
                    one = c < CHUNKS - 1
                    two = c < CHUNKS - 2
                    z_copy(n, k)
                    if k == 0 and one:
                        scale(c + 1)
                    if k == 1 and one:
                        time_clip(c + 1)
                    if k == 0 and two:
                        dve.wait_ge(x_loaded[c + 2], 16 * QUAD)
                        statistics(c + 2, range(0, 2))
                    if k == 1 and two:
                        statistics(c + 2, range(4, 6))
                    if k == 2 and two:
                        mean_parts()
                    z_square(2 * n)
                    if k == 0 and one:
                        bias(c + 1)
                    if k == 2 and c == CHUNKS - 2:
                        dve.wait_ge(q_ready, CHUNKS)
                        q_square(0)
                    if not one and k == 3:
                        dve.wait_ge(node_a, 3)
                        step.go(dve.reciprocal(tmp65, ny2))
                    if k == 0 and two:
                        statistics(c + 2, range(2, 4))
                    if k == 1 and two:
                        statistics(c + 2, range(6, CT))
                    if k == 2 and two:
                        mean_square()
                    z_square(2 * n + 1)
                    if k == 0 and one:
                        time_shift(c + 1)
                    if k == 2 and c == CHUNKS - 2:
                        q_square(1)
                    if not one and k == 1:
                        q_sum()
                    if not one and k == 2:
                        y_floor()
                    if k == 2 and two:
                        variance()
                        variance_eps()
                    if k == 3 and CHUNKS - 4 < c < CHUNKS - 1:
                        turn_unit(0, c - (CHUNKS - 3))

            dve.wait_ge(z_squared, TILES)
            dve.tensor_scalar(n2, n2, NORM_FLOOR2, None, ALU.max).then_inc(node_v, 1)
            dve.wait_ge(node_a, 3)
            step.settle()
            step.go(dve.scalar_tensor_tensor(out=c_, in0=c_, scalar=ACOSH_MIN, in1=tmp65, op0=ALU.max, op1=ALU.mult))
            dve.wait_ge(node_a, 4)
            step.settle()
            step.go(dve.tensor_tensor(a_, c_, n_, ALU.mult))
            dve.wait_ge(node_v, 2)
            step.go(dve.reciprocal(tmp64, n_))
            step.settle(1)
            step(dve.tensor_scalar(a_, a_, ACOSH_MIN, None, ALU.max))
            step(dve.tensor_tensor(r_, a_, tmp64, ALU.mult))
            dve.tensor_tensor(tv, r_, xz_t[:, :, D - 1], ALU.mult).then_inc(r_ready, 1)
            dve.wait_ge(r_ready, 1)
            step.go(dve.tensor_reduce(sc[:, 1:2], tv, AX.X, ALU.min))
            dve.tensor_reduce(sc[:, 0:1], tv, AX.X, ALU.max)
            dve.tensor_reduce(sc[:, 2:3], a_, AX.X, ALU.max)
            step.settle()
            dve.tensor_scalar(sc[:, 1:2], sc[:, 1:2], -1.0, None, ALU.mult).then_inc(node_v, 1)
            dve.wait_ge(node_p, 1)
            step(dve.tensor_reduce(sc[0:3, 3:4], pm2[0:3, 0:P], AX.X, ALU.max))
            dve.tensor_scalar(sc[0:3, 5:8], ident[0:3, 0:3], sc[0:3, 3:4], None, ALU.mult).then_inc(node_v, 1)
            dve.wait_ge(node_p, 2)
            dve.tensor_scalar(sc[:, 4:5], pm2[:, P:P + 1], -1.0, None, ALU.mult).then_inc(node_v, 1)
            step(dve.reciprocal(xz_t[:, :, D - 1], r_))
            step(dve.tensor_reduce(sc[:, 12:13], pm2[:, P:P + 2], AX.X, ALU.add))
            step(dve.scalar_tensor_tensor(out=sc[:, 12:13], in0=pm2[:, P + 2:P + 3], scalar=WIDE_T / WIDE_NORM,
                                          in1=sc[:, 12:13], op0=ALU.mult, op1=ALU.max))
            dve.tensor_scalar(wide_flag[:, :], sc[:, 12:13], WIDE_T, None, ALU.is_gt).then_inc(flag_ready, 1)

            def split_tiles(ts):
                for t in ts:
                    if not high_by_act(t):
                        dve.tensor_scalar(g[:, t, 0, :], xz_t[:, t, :], gr[:, t:t + 1], None, ALU.mult)\
                           .then_inc(split_high, 1)
                for t in ts:
                    if high_by_act(t):
                        dve.wait_ge(split_high_a, highs(t, True))
                    else:
                        dve.wait_ge(split_high, highs(t, False))
                    dve.scalar_tensor_tensor(out=g[:, t, 1, :], in0=xz_t[:, t, :], scalar=gr[:, t:t + 1],
                                             in1=g[:, t, 0, :], op0=ALU.mult, op1=ALU.subtract).then_inc(split, 1)

            def root(own, dst, arg, half):
                dve.tensor_scalar(dst.bitcast(I32), arg.bitcast(I32), 0.5, SQRT_MAGIC, ALU.mult, ALU.add)
                own(dve.tensor_scalar(half, arg, 0.5, None, ALU.mult))
                rec = e8[:, 15, 0:dst.shape[1]]
                for _ in range(3):
                    own(dve.reciprocal(rec, dst))
                    own(dve.tensor_tensor(rec, rec, half, ALU.mult))
                    own(dve.scalar_tensor_tensor(out=dst, in0=dst, scalar=0.5, in1=rec, op0=ALU.mult, op1=ALU.add))

            def copy_acc(j, b, serial=False, halved=False):
                dve.wait_ge(multiplied, (j + 1) * TILES)
                if not serial:
                    after(dve, projected, j * RT)
                for h in range(DH - 1 if halved else DH):
                    dve.tensor_copy(uT[:, h, :], acc[b][h][:, :]).then_inc(acc_copied, 1)

            def normalise(j, b, ks, serial=False):
                for pair in range(ks[0], ks[-1], 2):
                    own = Chain(dve, v_norm, j * N_NORM + N_NORM // 4 * pair)
                    two = (pair, pair + 1)
                    empty, den, rden = [e8[:, i, pair:pair + 2] for i in (1, 2, 3)]
                    for i, k in enumerate(two):
                        dve.wait_ge(projected, j * RT + (k + 1))
                        own.go(dve.tensor_scalar(empty[:, i:i + 1], hp[k][:, D:D + 1], 0.0, None, ALU.is_equal))
                    for i, k in enumerate(two):
                        own.settle()
                        ins = dve.tensor_tensor(den[:, i:i + 1], hp[k][:, D:D + 1], empty[:, i:i + 1], ALU.add)
                    own(ins)
                    own(dve.reciprocal(rden, den))
                    if not serial:
                        after(dve, tanh_ready, j * RT)
                    for i, k in enumerate(two):
                        dve.scalar_tensor_tensor(out=hrow[:, k, :], in0=hmean[:, :], scalar=empty[:, i:i + 1],
                                                 in1=hp[k][:, 0:D], op0=ALU.mult, op1=ALU.add).then_inc(hp_read, 1)
                    for i, k in enumerate(two):
                        dve.wait_ge(hp_read, j * RT + (k + 1))
                        dve.tensor_scalar(erow[b][:, k, :], hrow[:, k, :], rden[:, i:i + 1], 0.0, ALU.mult, ALU.min)\
                           .then_inc(neg_ready, 1)
                        own.go(dve.tensor_scalar(hrow[:, k, :], hrow[:, k, :], rden[:, i:i + 1], 0.0,
                                                 ALU.mult, ALU.max))
                    own.settle()
                    assert own.n == N_NORM // 2

            def elu(j, b):
                for k in range(RT):
                    dve.wait_ge(exp_ready, j * RT + (k + 1))
                    dve.scalar_tensor_tensor(out=hrow[:, k, :], in0=erow[b][:, k, :], scalar=-1.0, in1=hrow[:, k, :],
                                             op0=ALU.add, op1=ALU.add).then_inc(elu_ready, 1)

            def elu_norm(j):
                own = Chain(dve, v_root, j * N_ROOT)
                dve.wait_ge(elu_squared, (j + 1) * RT)
                own.go(dve.tensor_scalar(e8[:, 4, 0:RT], e8[:, 0, 0:RT], NORM_FLOOR2, None, ALU.max))
                own(dve.tensor_scalar(e8[:, 4, RT:2 * RT], e8[:, 0, 0:RT], 1.0, None, ALU.add))
                root(own, e8[:, 7, :], e8[:, 4, :], e8[:, 11, :])
                dve.tensor_tensor(e8[:, 5, 0:RT], e8[:, 7, 0:RT], e8[:, 7, RT:2 * RT], ALU.add).then_inc(ln_arg, 1)
                assert own.n == N_ROOT

            def tanh_scale(j):
                own = Chain(dve, v_scale, j * N_SCALE)
                own(dve.reciprocal(e8[:, 11, 0:RT], e8[:, 7, 0:RT]))
                own(dve.tensor_scalar(e8[:, 11, 0:RT], e8[:, 11, 0:RT], 0.5, None, ALU.mult))
                dve.wait_ge(ln_ready, j + 1)
                dve.scalar_tensor_tensor(out=e8[:, 6, 0:RT], in0=e8[:, 5, 0:RT], scalar=ACOSH_MIN,
                                         in1=e8[:, 11, 0:RT], op0=ALU.max, op1=ALU.mult).then_inc(scale_ready, 1)
                assert own.n == N_SCALE

            def sigmoid(j, b):
                own = Chain(dve, v_sig, j * N_SIG)
                for k in range(RT + 1):
                    if k < RT:
                        dve.wait_ge(tanh_ready, j * RT + (k + 1))
                        own.go(dve.tensor_scalar(erow[b][:, k, :], erow[b][:, k, :], 0.5, 0.5, ALU.mult, ALU.add))
                    if k > 0:
                        own.settle(1 if k < RT else 0)
                        row = erow[b][:, k - 1, 1:D]
                        own.go(dve.scalar_tensor_tensor(out=junk_v[:, k % 2, 0:D - 1], in0=row, scalar=1.0, in1=row,
                                                        op0=ALU.mult, op1=ALU.mult, accum_out=e8[:, 9, k - 1:k]))
                own.settle()
                own(dve.tensor_scalar(e8[:, 9, 0:RT], e8[:, 9, 0:RT], NORM_FLOOR2, None, ALU.max))
                root(own, e8[:, 8, 0:RT], e8[:, 9, 0:RT], e8[:, 14, 0:RT])
                dve.reciprocal(e8[:, 14, 0:RT], e8[:, 8, 0:RT]).then_inc(norm_ready, 1)
                assert own.n == N_SIG

            def finish(j, pair, b):
                own = Chain(dve, v_fin, j * N_FIN)
                dve.wait_ge(norm_ready, j + 1)
                dve.wait_ge(cosh_ready, j + 1)
                dve.wait_ge(xt_loaded[b], (pair + 1) * 16)
                ex, inv, sh, ch, rn = [e8[:, i, 0:RT] for i in (10, 11, 12, 13, 14)]
                own(dve.reciprocal(inv, ex))
                own.go(dve.tensor_tensor(sh, ex, inv, ALU.subtract))
                own.go(dve.tensor_tensor(ch, ex, inv, ALU.add))
                own.settle(1)
                own(dve.scalar_tensor_tensor(out=sh, in0=sh, scalar=0.5, in1=rn, op0=ALU.mult, op1=ALU.mult))
                for k in range(RT):
                    dve.scalar_tensor_tensor(out=xt[b][:, k, 1:D], in0=erow[b][:, k, 1:D], scalar=sh[:, k:k + 1],
                                             in1=xt[b][:, k, 1:D], op0=ALU.mult, op1=ALU.add)
                dve.scalar_tensor_tensor(out=xt[b][:, :, 0], in0=ch, scalar=0.5, in1=xt[b][:, :, 0],
                                         op0=ALU.mult, op1=ALU.add).then_inc(rows_ready, 1)
                assert own.n == N_FIN

            def mean_row():
                dve.wait_ge(node_sum, UNITS)
                step(dve.tensor_reduce(sc[:, 10:11], pm[:, 0:3], AX.X, ALU.add))
                step(dve.tensor_reduce(sc[:, 11:12], pm2[:, 0:3], AX.X, ALU.add))
                dve.tensor_scalar(diag[:, 0, :], ones[:, :], sc[:, 10:11], 1.0 / N, ALU.mult, ALU.mult)
                dve.tensor_scalar(diag[:, 1, :], ones[:, :], sc[:, 11:12], 1.0 / N, ALU.mult, ALU.mult)\
                   .then_inc(node_v, 1)

            def main(ib, pair, b, prev, prev2, last=False):
                for u in range(UNITS):
                    turn_unit(ib, u)
                    if isinstance(ib, int) and ib == 1 and u == 3:
                        mean_row()
                    if isinstance(ib, int) and ib == 1 and u == 4:
                        dve.wait_ge(node_p, 3)
                        dve.tensor_copy(hmean[:, :], pm[:, D:2 * D]).then_inc(node_v, 1)
                        dve.wait_ge(node_v, 9)
                    if prev2 and u == 1:
                        elu_norm(ib - 2)
                    if prev and u == 3:
                        copy_acc(ib - 1, 1 - b)
                    if prev2 and u == 3:
                        tanh_scale(ib - 2)
                    if prev and u == 4:
                        normalise(ib - 1, 1 - b, range(RT) if last else (0, 1))
                    if prev2 and u == 5:
                        sigmoid(ib - 2, b)
                    if prev and u == (5 if last else 7):
                        elu(ib - 1, 1 - b)
                    if prev and u == 6 and not last:
                        normalise(ib - 1, 1 - b, (2, 3))
                    if prev2 and u == (6 if last else 7):
                        finish(ib - 2, pair - 1, b)
                    if last and u == 6:
                        elu_norm(ib - 1)
                    if last and u == 7:
                        tanh_scale(ib - 1)

            dve.wait_ge(flag_ready, 1)
            is_wide = dve.value_load(wide_flag[0:1, 0:1])
            with dve.If(is_wide == 0):
                dve.wait_ge(node_a, 5)
                step(dve.scalar_tensor_tensor(out=tmp64, in0=a_, scalar=1.0, in1=w_, op0=ALU.max, op1=ALU.mult))
                step(dve.tensor_scalar(tmp64.bitcast(I32), tmp64.bitcast(I32), EXP_MASK, None, ALU.bitwise_and))
                dve.tensor_scalar(beta, tmp64, BETA, None, ALU.mult).then_inc(beta_ready, 1)
                step(dve.tensor_scalar(tmp65.bitcast(I32), tmp64.bitcast(I32), -1.0, INVERSE_BITS, ALU.mult, ALU.add))
                step(dve.tensor_tensor(gs, w_, tmp65, ALU.mult))
                dve.tensor_tensor(gr, gs, r_, ALU.mult).then_inc(w_ready, 1)
                dve.wait_ge(w_ready, 1)

                N_WIDE = QTR + 1 + 2 * UNITS + 2 * 2 * TILES + (TILES - 1) + 2

                def wide_block(j):
                    own = Chain(dve, v_wide, j * N_WIDE)

                    def turn_wide(u):
                        src = raw[u // 2].bitcast(U32).rearrange("p (g h m w) -> p h m g w", h=2, m=UM, w=B32)
                        own(dve.transpose(mT[0][:, :, :, :], src[:, u % 2]))

                    def logits(u, i):
                        mv = mT[0][:, :, :, :].bitcast(BF16)
                        edge = mv[:, i // 2, :, :].rearrange("p g (i e) -> p (g i) e", e=2)[:, :, i % 2]
                        t = u * UT + i
                        own(dve.tensor_scalar(fill, edge, 1.0, -MASK_FILL, ALU.subtract, ALU.mult))
                        own(dve.scalar_tensor_tensor(out=logit, in0=edge, scalar=tv[:, t:t + 1], in1=fill,
                                                     op0=ALU.mult, op1=ALU.add))

                    for q in range(QTR):
                        dve.wait_ge(adj_loaded[q], (j + (2 if q < NRAW else 1)) * (16 * QUAD))
                        own(dve.tensor_scalar(raw[q], raw[q], 0.0, None, ALU.is_gt))
                    own(dve.memset(best, -3.0e38))
                    for u in range(UNITS):
                        turn_wide(u)
                        for i in range(UT):
                            logits(u, i)
                            ins = dve.tensor_tensor(best, best, logit, ALU.max)
                            if u * UT + i < TILES - 1:
                                own(ins)
                    ins.then_inc(best_ready, 1)
                    dve.wait_ge(best_turned, j + 1)
                    own(dve.tensor_reduce(sc[:, 12:16], hp[0][:, :].rearrange("p (k n) -> p k n", k=RT), AX.X, ALU.max))
                    for k in range(RT):
                        ins = dve.tensor_scalar(diag_top[:, k * P:(k + 1) * P], ident[:, :], sc[:, 12 + k:13 + k], None,
                                                ALU.mult)
                    ins.then_inc(top_ready, 1)
                    dve.wait_ge(top_spread, j + 1)
                    own(dve.tensor_copy(top_row, hp[1][:, :]))
                    for u in range(UNITS):
                        turn_wide(u)
                        for i in range(UT):
                            t = u * UT + i
                            logits(u, i)
                            if t >= 2:
                                dve.wait_ge(multiplied, j * TILES + (t - 1))
                            dve.tensor_tensor(weight[t % 2], logit, top_row, ALU.subtract).then_inc(logit_ready, 1)
                    dve.sem_inc(wide_free, 1)
                    assert own.n == N_WIDE
                    copy_acc(j, 0, serial=True)
                    normalise(j, 0, range(RT), serial=True)
                    elu(j, 0)
                    elu_norm(j)
                    tanh_scale(j)
                    sigmoid(j, 0)
                    finish(j, j, 0)

                def column_reciprocals():
                    step(dve.reciprocal(tmp65, gs))
                    step(dve.tensor_copy(cf[:, :, 0], tmp65))
                    step(dve.tensor_tensor(tmp65, tmp65, cf[:, :, 0], ALU.subtract))
                    step(dve.tensor_copy(cf[:, :, 1], tmp65))
                    dve.tensor_tensor(cf[:, :, 2], tmp65, cf[:, :, 1], ALU.subtract).then_inc(cf_ready, 1)

                for u in range(UNITS):
                    if u == 0:
                        split_tiles(range(0, 1))
                        split_tiles(range(1, UM))
                        column_reciprocals()
                    else:
                        split_tiles(range(u * UT, u * UT + UM))
                    split_tiles(range(u * UT + UM, (u + 1) * UT))
                    if u >= 2:
                        turn_unit(0, u)
                dve.wait_ge(split, TILES)
                main(1, 0, 1, True, False)
                with dve.Fori(0, BLOCKS // 2 - 2) as k:
                    for b in range(2):
                        main(2 * k + 2 + b, k + 1, b, True, True)
                main(BLOCKS - 2, BLOCKS // 2 - 1, 0, True, True)
                main(BLOCKS - 1, BLOCKS // 2 - 1, 1, True, True, last=True)
                j = BLOCKS - 2
                sigmoid(j, 0)
                copy_acc(j + 1, 1, halved=True)
                finish(j, j // 2, 0)
                j = BLOCKS - 1
                normalise(j, 1, range(RT))
                elu(j, 1)
                elu_norm(j)
                tanh_scale(j)
                sigmoid(j, 1)
                finish(j, j // 2, 1)
            with dve.Else():
                dve.wait_ge(is_set, NRAW)
                dve.wait_ge(transposed, 2)
                dve.memset(hmean[:, :], 0.0).then_inc(v_wide_set, 1)
                for t in range(TILES):
                    dve.tensor_scalar(h32[:, t, :], xz_t[:, t, :], r_[:, t:t + 1], None, ALU.mult)\
                       .then_inc(v_wide_set, 1)
                dve.wait_ge(v_wide_set, TILES + 1)
                dve.sem_inc(wide_free, 1)
                with dve.Fori(0, BLOCKS) as j:
                    wide_block(j)


_INS = ["x", "adj", "L0_gnn_W_gcn", "L0_gnn_W_att", "L0_gnn_a_att"]


def kernel(**inputs):
    import numpy as _np
    import concourse.bacc as _bacc
    from concourse import mybir as _mybir
    from concourse.bass_utils import run_bass_kernel_spmd as _run

    nc = _bacc.Bacc("TRN2", target_bir_lowering=False, num_devices=1)
    arrays, args = {}, []
    for name in _INS:
        a = _np.ascontiguousarray(inputs[name])
        arrays[f"in_{name}"] = a
        args.append(nc.dram_tensor(f"in_{name}", a.shape, _mybir.dt.from_np(a.dtype), kind="ExternalInput").ap())
    args.append(nc.dram_tensor("out_rows", inputs["x"].shape, _mybir.dt.float32, kind="ExternalOutput").ap())
    gnn_kernel(nc, *args)
    r = _run(nc, [arrays], core_ids=[0])
    return r.results[0]["out_rows"]
```
